# Optimizing a Trainium2 kernel written in Bass

```python
import numpy as np
import jax
import jax.numpy as jnp

def _softmax(x, axis=-1):
    return jax.nn.softmax(x, axis=axis)

def _gelu(x):
    return jax.nn.gelu(x, approximate=True)

def _silu(x):
    return jax.nn.silu(x)

def _sigmoid(x):
    return jax.nn.sigmoid(x)

def _layernorm(x, axis=-1, eps=1e-05):
    m = jnp.mean(x, axis=axis, keepdims=True)
    v = jnp.var(x, axis=axis, keepdims=True)
    return (x - m) / jnp.sqrt(v + eps)

def _scatter_add(tgt, idx, src, axis=0):
    return tgt.at[idx].add(src)

def _segment_sum(src, seg, n):
    return jax.ops.segment_sum(src, seg, n)
kernel_name = 'mk_gnn_ffn_d2_gnn_r8_e0aa8f'

def setup_inputs(seed: int=0):
    np.random.seed(seed)
    _w = jnp.asarray

    def _rec_inputs():
        import jax
        import jax.numpy as jnp
        _gk = jax.random.key(seed)
        x = -0.0002117 + 1 * jax.random.normal(jax.random.fold_in(_gk, 1), (3125, 1024), jnp.float32)
        _s = jax.random.randint(jax.random.fold_in(_gk, 2), (25000,), 0, 3125, jnp.int32)
        _d = jax.random.randint(jax.random.fold_in(_gk, 3), (25000,), 0, 3125, jnp.int32)
        _loop = jnp.arange(3125, dtype=jnp.int32)
        src = jnp.concatenate([_s, _d, _loop])
        dst = jnp.concatenate([_d, _s, _loop])
        _o = jnp.argsort(dst, stable=True)
        src = src[_o]
        dst = dst[_o]
        return (x, src, dst)
    x, src, dst = _rec_inputs()

    def _L0_gnn_setup():
        import jax, jax.numpy as jnp
        import numpy as np
        N = 3125
        E = 50000
        H = 4
        C = 256
        D_IN = 1024
        NEG_SLOPE = 0.2
        key = jax.random.key(seed)
        k1, k2, k3, k4, k5, k6 = jax.random.split(key, 6)
        x = jax.random.normal(k1, (N, D_IN), dtype=jnp.float32)
        edge_index = jax.random.randint(k2, (2, E), 0, N, dtype=jnp.int64)
        scale = 1.0 / np.sqrt(D_IN)
        W = jax.random.normal(k3, (D_IN, H * C), dtype=jnp.float32) * scale
        att_src = jax.random.normal(k4, (H, C), dtype=jnp.float32) * 0.1
        att_dst = jax.random.normal(k5, (H, C), dtype=jnp.float32) * 0.1
        bias = jax.random.normal(k6, (H * C,), dtype=jnp.float32) * 0.01
        return {'x': x, 'edge_index': edge_index, 'W': W, 'att_src': att_src, 'att_dst': att_dst, 'bias': bias}
    _L0_gnn_all = _L0_gnn_setup()
    _L0_gnn_in = {k: v for k, v in _L0_gnn_all.items() if k in ('W', 'att_src', 'att_dst', 'bias')}
    del _L0_gnn_all

    def _L0_ffn_setup():
        import jax, jax.numpy as jnp
        import numpy as np
        DIM = 1024

        def _reference_tuple_inner(x, W_r, W_k, W_v, mu_r, mu_k):
            B, T, C = x.shape
            x_prev = jnp.concatenate([jnp.zeros((B, 1, C), x.dtype), x[:, :-1, :]], axis=1)
            xr = mu_r * x + (1.0 - mu_r) * x_prev
            xk = mu_k * x + (1.0 - mu_k) * x_prev
            r = jax.nn.sigmoid(jnp.einsum('btc,dc->btd', xr, W_r))
            k = jnp.einsum('btc,dc->btd', xk, W_k)
            k_act = jnp.square(jax.nn.relu(k))
            out = r * jnp.einsum('btc,dc->btd', k_act, W_v)
            new_state = x[:, -1, :]
            return (out, new_state)
        key = jax.random.key(seed)
        ks = jax.random.split(key, 6)
        B, T, C = (8, 256, DIM)
        x = jax.random.normal(ks[0], (B, T, C), dtype=jnp.float32)
        s = 1.0 / np.sqrt(C)
        W_r = jax.random.uniform(ks[1], (C, C), jnp.float32, -s, s)
        W_k = jax.random.uniform(ks[2], (C, C), jnp.float32, -s, s)
        W_v = jax.random.uniform(ks[3], (C, C), jnp.float32, -s, s)
        mu_r = jax.random.uniform(ks[4], (C,), jnp.float32)
        mu_k = jax.random.uniform(ks[5], (C,), jnp.float32)
        return {'x': x, 'W_r': W_r, 'W_k': W_k, 'W_v': W_v, 'mu_r': mu_r, 'mu_k': mu_k}
    _L0_ffn_all = _L0_ffn_setup()
    _L0_ffn_in = {k: v for k, v in _L0_ffn_all.items() if k in ('W_r', 'W_k', 'W_v', 'mu_r', 'mu_k')}
    del _L0_ffn_all

    def _L1_gnn_setup():
        import jax, jax.numpy as jnp
        import numpy as np
        N = 2500
        E = 40000
        D_IN = 1024
        D_OUT = 1024
        key = jax.random.key(seed)
        k1, k2, k3, k4 = jax.random.split(key, 4)
        x = jax.random.normal(k1, (N, D_IN), dtype=jnp.float32)
        edge_index = jax.random.randint(k2, (2, E), 0, N, dtype=jnp.int64)
        W = jax.random.normal(k3, (D_OUT, D_IN), dtype=jnp.float32) * (1.0 / np.sqrt(D_IN))
        b = jax.random.normal(k4, (D_OUT,), dtype=jnp.float32) * 0.01
        return {'x': x, 'edge_index': edge_index, 'W': W, 'b': b}
    _L1_gnn_all = _L1_gnn_setup()
    _L1_gnn_in = {k: v for k, v in _L1_gnn_all.items() if k in ('W', 'b')}
    del _L1_gnn_all

    def _L1_ffn_setup():
        import jax, jax.numpy as jnp
        import numpy as np
        NUM_OPS, B, T, D = (8, 8, 512, 1024)
        key = jax.random.key(seed)
        k1, k2, k3, k4 = jax.random.split(key, 4)
        x = jax.random.normal(k1, (B, T, D), dtype=jnp.float32)
        W = jax.random.normal(k2, (NUM_OPS, D, D), dtype=jnp.float32) * 0.02
        b = jnp.zeros((NUM_OPS, D), dtype=jnp.float32)
        logits = 0.001 * jax.random.normal(k3, (NUM_OPS,), dtype=jnp.float32)
        u = jax.random.uniform(k4, (NUM_OPS,), dtype=jnp.float32, minval=1e-06, maxval=1.0 - 1e-06)
        return {'x': x, 'W': W, 'b': b, 'logits': logits, 'u': u}
    _L1_ffn_all = _L1_ffn_setup()
    _L1_ffn_in = {k: v for k, v in _L1_ffn_all.items() if k in ('W', 'b', 'logits', 'u')}
    del _L1_ffn_all
    return {'x': x, 'src': src, 'dst': dst, 'L0_gnn_W': _L0_gnn_in['W'], 'L0_gnn_att_src': _L0_gnn_in['att_src'], 'L0_gnn_att_dst': _L0_gnn_in['att_dst'], 'L0_gnn_bias': _L0_gnn_in['bias'], 'L0_ffn_W_r': _L0_ffn_in['W_r'], 'L0_ffn_W_k': _L0_ffn_in['W_k'], 'L0_ffn_W_v': _L0_ffn_in['W_v'], 'L0_ffn_mu_r': _L0_ffn_in['mu_r'], 'L0_ffn_mu_k': _L0_ffn_in['mu_k'], 'L1_gnn_W': _L1_gnn_in['W'], 'L1_gnn_b': _L1_gnn_in['b'], 'L1_ffn_W': _L1_ffn_in['W'], 'L1_ffn_b': _L1_ffn_in['b'], 'L1_ffn_logits': _L1_ffn_in['logits'], 'L1_ffn_u': _L1_ffn_in['u']}

def reference(x, src, dst, L0_gnn_W, L0_gnn_att_src, L0_gnn_att_dst, L0_gnn_bias, L0_ffn_W_r, L0_ffn_W_k, L0_ffn_W_v, L0_ffn_mu_r, L0_ffn_mu_k, L1_gnn_W, L1_gnn_b, L1_ffn_W, L1_ffn_b, L1_ffn_logits, L1_ffn_u):
    import jax
    import jax.numpy as jnp

    def _L0_gnn_ref(x, edge_index, W, att_src, att_dst, bias):
        import jax, jax.numpy as jnp
        import numpy as np
        N = 3125
        E = 50000
        H = 4
        C = 256
        D_IN = 1024
        NEG_SLOPE = 0.2
        xp = (x @ W).reshape(N, H, C)
        a_src = jnp.einsum('nhc,hc->nh', xp, att_src)
        a_dst = jnp.einsum('nhc,hc->nh', xp, att_dst)
        loops = jnp.arange(N, dtype=edge_index.dtype)
        src = jnp.concatenate([edge_index[0], loops])
        dst = jnp.concatenate([edge_index[1], loops])
        e = jax.nn.leaky_relu(a_src[src] + a_dst[dst], NEG_SLOPE)
        m = jax.ops.segment_max(e, dst, num_segments=N)
        ee = jnp.exp(e - m[dst])
        z = jax.ops.segment_sum(ee, dst, num_segments=N)
        alpha = ee / z[dst]
        msgs = xp[src] * alpha[:, :, None]
        out = jax.ops.segment_sum(msgs, dst, num_segments=N)
        out = out.reshape(N, H * C) + bias
        return jax.nn.relu(out)

    def _L0_ffn_ref(x, W_r, W_k, W_v, mu_r, mu_k):
        import jax, jax.numpy as jnp
        import numpy as np
        DIM = 1024

        def _reference_tuple_inner(x, W_r, W_k, W_v, mu_r, mu_k):
            B, T, C = x.shape
            x_prev = jnp.concatenate([jnp.zeros((B, 1, C), x.dtype), x[:, :-1, :]], axis=1)
            xr = mu_r * x + (1.0 - mu_r) * x_prev
            xk = mu_k * x + (1.0 - mu_k) * x_prev
            r = jax.nn.sigmoid(jnp.einsum('btc,dc->btd', xr, W_r))
            k = jnp.einsum('btc,dc->btd', xk, W_k)
            k_act = jnp.square(jax.nn.relu(k))
            out = r * jnp.einsum('btc,dc->btd', k_act, W_v)
            new_state = x[:, -1, :]
            return (out, new_state)
        return _reference_tuple_inner(x, W_r, W_k, W_v, mu_r, mu_k)[0]

    def _L1_gnn_ref(x, edge_index, W, b):
        import jax, jax.numpy as jnp
        import numpy as np
        N = 2500
        E = 40000
        D_IN = 1024
        D_OUT = 1024
        num_nodes = x.shape[0]
        self_idx = jnp.arange(num_nodes, dtype=edge_index.dtype)
        ei = jnp.concatenate([edge_index, jnp.stack([self_idx, self_idx], axis=0)], axis=1)
        row, col = (ei[0], ei[1])
        h = jnp.einsum('nd,od->no', x, W) + b
        deg = jnp.zeros((num_nodes,), dtype=h.dtype).at[row].add(1.0)
        deg_inv_sqrt = deg ** (-0.5)
        norm = deg_inv_sqrt[row] * deg_inv_sqrt[col]
        msg = norm[:, None] * h[col]
        out = jax.ops.segment_sum(msg, row, num_segments=num_nodes)
        return out

    def _L1_ffn_ref(x, W, b, logits, u):
        import jax, jax.numpy as jnp
        import numpy as np
        NUM_OPS, B, T, D = (8, 8, 512, 1024)
        gumbel = -jnp.log(-jnp.log(u))
        idx = jnp.argmax(jax.nn.log_softmax(logits) + gumbel)
        out = jnp.einsum('btd,de->bte', x, W[idx]) + b[idx]
        return out
    edge_index = jnp.stack([src, dst])
    x = x + _L0_gnn_ref(_layernorm(x, axis=-1), edge_index, L0_gnn_W, L0_gnn_att_src, L0_gnn_att_dst, L0_gnn_bias)
    x = x + _L0_ffn_ref(_layernorm(x, axis=-1)[None], L0_ffn_W_r, L0_ffn_W_k, L0_ffn_W_v, L0_ffn_mu_r, L0_ffn_mu_k)[0]
    x = x + _L1_gnn_ref(_layernorm(x, axis=-1), edge_index, L1_gnn_W, L1_gnn_b)
    x = x + _L1_ffn_ref(_layernorm(x, axis=-1)[None], L1_ffn_W, L1_ffn_b, L1_ffn_logits, L1_ffn_u)[0]
    return x

_drawn_inputs = setup_inputs


def setup_inputs(seed=0):
    import zlib

    import numpy as np

    out = dict(_drawn_inputs(seed))
    spreads = {'L1_ffn_b': (0.0, 0.1)}
    factors = {'L0_gnn_bias': 6.901, 'L0_ffn_W_r': 3.328, 'L0_ffn_mu_r': 6.852, 'L1_gnn_b': 6.566}
    for name, (base, spread) in spreads.items():
        noise = np.random.default_rng([zlib.crc32(name.encode()), seed]).standard_normal(out[name].shape)
        drawn = base * np.exp(spread * noise) if base else spread * noise
        out[name] = jnp.asarray(drawn.astype(out[name].dtype))
    for name, factor in factors.items():
        out[name] = (out[name] * factor).astype(out[name].dtype)
    return out
```

```python
import concourse.bass as bass
from concourse import mybir
from contextlib import ExitStack

F32 = mybir.dt.float32
F32R = mybir.dt.float32r
BF16 = mybir.dt.bfloat16
U16 = mybir.dt.uint16
U32 = mybir.dt.uint32
I32 = mybir.dt.int32
ALU = mybir.AluOpType
ACT = mybir.ActivationFunctionType
AXX = mybir.AxisListType.X

NODES = 3125
EDGES = 53125
D = 1024
P = 125
NB = NODES // P
KC = D // 128
HALF = 512
HEADS = 4
C = D // HEADS
SLOPE = 0.2
EPS = 1e-5
WIDE = 112
ROWS_SEM = 32
MASKED = -3.0e38

EG = EDGES // P
SG = 5
STEPS = EG // SG
SE = SG * P
EARLIER = 4096.0
SPARE = NODES * NODES
CELLS = NODES * (NODES + 1)


def rows_dma(eng, out, in_, sem):
    eng.dma_start(out[0:WIDE], in_[0:WIDE]).then_inc(sem, 16)
    eng.dma_start(out[WIDE:P], in_[WIDE:P]).then_inc(sem, 16)


def hold(eng, held, sem, value):
    eng.wait_ge(sem, value)
    eng.sem_inc(held, 1)


def at(base, first):
    return base[bass.ds(first, P)] if not isinstance(first, int) else base[first:first + P]


class Semaphores:

    def __init__(self, nc):
        self.nc, self.taken = nc, []

    def __call__(self, name):
        self.taken.append(self.nc.alloc_semaphore(name=name))
        return self.taken[-1]

    def end_stage(self):
        self.nc.clear_and_free_semaphores(self.taken)
        self.nc.all_engine_barrier()
        self.taken = []


def make_identity(nc, ident, made, step):
    nc.gpsimd.memset(ident[:, :], 0.0).then_inc(step, 1)
    nc.gpsimd.wait_ge(step, 1)
    nc.gpsimd.affine_select(out=ident[:, :], in_=ident[:, :], compare_op=ALU.not_equal, fill=1.0, base=0,
                            pattern=[[-1, 128]], channel_multiplier=1).then_inc(made, 1)


def build_counts(nc, sem, ident, src, dst, key_rows, counts_flat):
    with ExitStack() as ctx:
        def sb(name, shape, dt):
            return ctx.enter_context(nc.sbuf_tensor("cnt_" + name, shape, dt))

        zero = sb("zero", [P, NODES], U16)
        one = sb("one", [P, NB], U16)
        src_i = sb("src_i", [P, EG], I32)
        dst_i = sb("dst_i", [P, EG], I32)
        key = sb("key", [P, EG], F32)
        key_t = sb("key_t", [P, 4, P], F32)
        weight = sb("weight", [P, SG, SE], F32)
        slot_i = sb("slot_i", [P, SG], I32)
        slot = sb("slot", [P, SG], F32)
        row = sb("row", [P, 2, SE], F32)
        junk = sb("junk", [P, SG, SE], BF16)
        mine = sb("mine", [P, 2, SG], F32)
        found = sb("found", [P, 2, SG], F32)
        first = sb("first", [P, 2, SG], F32)
        shifted = sb("shifted", [P, 2, SG], F32)
        chosen = sb("chosen", [P, 2, SG], F32)
        cell = sb("cell", [P, 2, SG], I32)
        add = sb("add", [P, 2, SG], U16)
        turned = ctx.enter_context(nc.psum_tensor("cnt_turned", [128, 4, 128], F32))

        edges_in = sem("edges_in")
        zero_made = sem("zero_made")
        zeroed = sem("zeroed")
        diagonal = sem("diagonal")
        keys_made = sem("keys_made")
        key_turned = sem("key_turned")
        key_copied = sem("key_copied")
        key_stored = sem("key_stored")
        weight_set = sem("weight_set")
        weight_made = sem("weight_made")
        slot_made = sem("slot_made")
        slot_cast = sem("slot_cast")
        row_in = [sem("row_in0"), sem("row_in1")]
        mine_made = sem("mine_made")
        compared = sem("compared")
        first_made = sem("first_made")
        shift_made = sem("shift_made")
        chosen_made = sem("chosen_made")
        cells_made = sem("cells_made")
        scattered = sem("scattered")
        issued = sem("issued")

        counts = counts_flat[0:NODES * NODES, :].rearrange("(b p s) o -> p b (s o)", p=P, s=NODES)
        diag = counts_flat[:, :].rearrange("(p b s) o -> p b (s o)", b=NB, s=NODES + 1)[:, :, 0:1]
        chunks = [(c, min(P, EG - c * P)) for c in range(4)]

        with nc.Block() as block:
            @block.sync
            def _(sp):
                rows_dma(sp, src_i[:, :], src.rearrange("(p g) -> p g", p=P), edges_in)
                rows_dma(sp, dst_i[:, :], dst.rearrange("(p g) -> p g", p=P), edges_in)
                sp.wait_ge(zero_made, 2)
                rows_dma(sp, counts, zero[:, :].unsqueeze(1).broadcast_to([P, NB, NODES]), zeroed)
                rows_dma(sp, counts_flat[SPARE:CELLS, :].rearrange("(p n) o -> p (n o)", p=P), zero[:, 0:NB], zeroed)
                sp.wait_ge(zeroed, 2 * ROWS_SEM)
                with nc.allow_non_contiguous_dma(reason="one cell of every row"):
                    rows_dma(sp, diag, one[:, :].unsqueeze(2), diagonal)
                sp.wait_ge(key_copied, 2)
                for c, n in chunks:
                    sp.dma_start(key_rows[c * P * P:c * P * P + n * P].rearrange("(g p) -> g p", p=P),
                                 key_t[0:n, c, :]).then_inc(key_stored, 16)
                sp.wait_ge(key_stored, 64)

                def load(i, j):
                    rows_dma(sp, row[:, j, :],
                             key_rows[bass.ds(i * (2 * SE) + j * SE, SE)].partition_broadcast(P)
                             if not isinstance(i, int) else
                             key_rows[(2 * i + j) * SE:(2 * i + j + 1) * SE].partition_broadcast(P), row_in[j])

                load(0, 0)
                load(0, 1)
                with sp.Fori(1, STEPS // 2) as i:
                    for j in range(2):
                        sp.wait_ge(compared, i * 2 + (j - 1))
                        load(i, j)
                sp.wait_ge(compared, STEPS - 2)
                load(STEPS // 2, 0)
                sp.wait_ge(diagonal, ROWS_SEM)

            @block.gpsimd
            def _(pool):
                nc.gpsimd.iota(slot_i[:, :], pattern=[[P, SG]], base=SPARE, channel_multiplier=1).then_inc(slot_made, 1)
                nc.gpsimd.memset(weight[:, :, :], EARLIER + 1.0).then_inc(weight_set, 1)
                pool.wait_ge(weight_set, 1)
                for g in range(SG):
                    nc.gpsimd.affine_select(out=weight[:, g, :], in_=weight[:, g, :], compare_op=ALU.is_gt, fill=1.0,
                                            base=g * P, pattern=[[-1, SE]],
                                            channel_multiplier=1).then_inc(weight_made, 1)
                pool.wait_ge(diagonal, ROWS_SEM)

                def scatter(i, j):
                    pool.wait_ge(cells_made, i * 2 + (j + 1))
                    pool.sem_inc(issued, 1)
                    if not (isinstance(i, int) and i == 0 and j == 0):
                        pool.wait_ge(scattered, (i * 2 + j) * (16 * SG))
                        pool.sem_inc(issued, 1)
                    for g in range(SG):
                        nc.gpsimd.indirect_dma_start(
                            counts_flat, bass.IndirectOffsetOnAxis(cell[:, j, g:g + 1], 0), add[:, j, g:g + 1], None,
                            compute_op=ALU.add).then_inc(scattered, 16)

                scatter(0, 0)
                scatter(0, 1)
                with pool.Fori(1, STEPS // 2) as i:
                    for j in range(2):
                        scatter(i, j)
                scatter(STEPS // 2, 0)
                pool.wait_ge(scattered, STEPS * SG * 16)

            @block.vector
            def _(dve):
                nc.vector.memset(zero[:, :], 0).then_inc(zero_made, 1)
                nc.vector.memset(one[:, :], 1).then_inc(zero_made, 1)
                dve.wait_ge(edges_in, 2 * ROWS_SEM)
                nc.vector.scalar_tensor_tensor(out=key[:, :], in0=dst_i[:, :], scalar=float(NODES), in1=src_i[:, :],
                                               op0=ALU.mult, op1=ALU.add).then_inc(keys_made, 1)
                dve.wait_ge(slot_made, 1)
                nc.vector.tensor_copy(slot[:, :], slot_i[:, :]).then_inc(slot_cast, 1)
                dve.wait_ge(key_turned, 1)
                nc.vector.tensor_copy(key_t[:, 0:3, :], turned[0:P, 0:3, 0:P]).then_inc(key_copied, 1)
                nc.vector.tensor_copy(key_t[0:EG - 3 * P, 3, :], turned[0:EG - 3 * P, 3, 0:P]).then_inc(key_copied, 1)
                dve.wait_ge(keys_made, 1)
                dve.wait_ge(slot_cast, 1)
                dve.wait_ge(weight_made, SG)

                def step(i, j):
                    n = i * 2 + (j + 1)
                    whole = isinstance(i, int)
                    g0 = (2 * i + j) * SG
                    nc.vector.tensor_copy(mine[:, j, :], key[:, g0:g0 + SG] if whole
                                          else key[:, bass.ds(i * (2 * SG) + j * SG, SG)]).then_inc(mine_made, 1)
                    dve.wait_ge(mine_made, n)
                    dve.wait_ge(row_in[j], i * ROWS_SEM + ROWS_SEM)
                    for g in range(SG):
                        last = nc.vector.scalar_tensor_tensor(out=junk[:, g, :], in0=row[:, j, :],
                                                              scalar=mine[:, j, g:g + 1], in1=weight[:, g, :],
                                                              op0=ALU.is_equal, op1=ALU.mult,
                                                              accum_out=found[:, j, g:g + 1])
                    last.then_inc(compared, 1)
                    dve.wait_ge(compared, n)
                    nc.vector.tensor_scalar(first[:, j, :], found[:, j, :], EARLIER, None, ALU.is_lt).then_inc(first_made, 1)
                    nc.vector.tensor_tensor(shifted[:, j, :], mine[:, j, :], slot[:, :], ALU.subtract).then_inc(shift_made, 1)
                    dve.wait_ge(first_made, n)
                    dve.wait_ge(shift_made, n)
                    nc.vector.tensor_tensor(chosen[:, j, :], shifted[:, j, :], first[:, j, :], ALU.mult).then_inc(chosen_made, 1)
                    if not (whole and i == 0):
                        dve.wait_ge(scattered, (i * 2 + (j - 1)) * (16 * SG))
                    nc.vector.tensor_tensor(add[:, j, :], found[:, j, :], first[:, j, :], ALU.mult)
                    dve.wait_ge(chosen_made, n)
                    nc.vector.tensor_tensor(cell[:, j, :], chosen[:, j, :], slot[:, :], ALU.add).then_inc(cells_made, 1)

                step(0, 0)
                step(0, 1)
                with dve.Fori(1, STEPS // 2) as i:
                    for j in range(2):
                        step(i, j)
                step(STEPS // 2, 0)

            @block.tensor
            def _(pe):
                pe.wait_ge(keys_made, 1)
                for c, n in chunks:
                    last = nc.tensor.transpose(turned[0:n, c, 0:P], key[:, c * P:c * P + n], ident[0:P, 0:P])
                last.then_inc(key_turned, 1)


class Turn:

    def __init__(self, i, j, unroll):
        self.i, self.j, self.unroll = i + j // unroll if j >= unroll else i, j % unroll, unroll

    def t(self, plus=0):
        return self.i * self.unroll + (self.j + plus)

    def after(self, n):
        return Turn(self.i, self.j + n, self.unroll)

    def slot(self, bufs):
        return self.j % bufs

    def use(self, bufs):
        return self.i * (self.unroll // bufs) + (self.j // bufs + 1)

    def row(self, step=P, plus=0):
        return self.i * (self.unroll * step) + (self.j * step + plus)

    def known(self):
        return self.i * self.unroll + self.j if isinstance(self.i, int) else None


UNROLL = 4
ROUNDS = (NB - 1) // UNROLL - 1


def all_tiles(eng, body):
    for j in range(UNROLL):
        body(Turn(0, j, UNROLL))
    with eng.Fori(1, ROUNDS) as i:
        for j in range(UNROLL):
            body(Turn(i, j, UNROLL))
    for t in range(ROUNDS * UNROLL, NB):
        body(Turn(t // UNROLL, t % UNROLL, UNROLL))


class Dense:
    weights, inputs, outputs = (), (), ()
    ahead = 2
    out_bufs = 2

    def __init__(self, nc, sem, ident, tag):
        self.nc, self.ident, self.tag, self.make_sem = nc, ident, tag, sem

    def sem(self, name):
        return self.make_sem(f"{self.tag}_{name}")

    def sb(self, name, shape, dt):
        return self.ctx.enter_context(self.nc.sbuf_tensor(f"{self.tag}_{name}", shape, dt))

    def ps(self, name, shape, dt):
        return self.ctx.enter_context(self.nc.psum_tensor(f"{self.tag}_{name}", shape, dt))

    def allocate(self): pass
    def weight(self, sp, s): return self.weights[s]
    def before_sync(self, sp): pass
    def before_scalar(self, act): pass
    def before_vector(self, dve): pass
    def prepare_vector(self, dve, turn): pass
    def prepare_gpsimd(self, pool, turn): pass
    def finish_scalar(self, act, turn, s): pass
    def finish_vector(self, dve, turn, s): pass
    def after_vector(self, dve): pass
    def after_gpsimd(self, pool): pass
    def after_tensor(self, pe): pass

    def slots(self, turn, s):
        S = len(self.weights)
        return turn.i * (UNROLL * S) + (turn.j * S + s + 1)

    def early(self, turn, s):
        return turn.known() is not None and turn.known() * len(self.weights) + s < 2

    def loaded(self, eng, name, turn):
        bufs = len(self.in_sem[name])
        eng.wait_ge(self.in_sem[name][turn.slot(bufs)], turn.use(bufs) * ROWS_SEM)

    def output_free(self, eng, name, turn):
        if turn.known() is None or turn.known() >= self.out_bufs:
            eng.wait_ge(self.out_sem[name][turn.slot(self.out_bufs)], (turn.use(self.out_bufs) - 1) * ROWS_SEM)

    def run(self):
        nc, S, tag = self.nc, len(self.weights), self.tag
        with ExitStack() as ctx:
            self.ctx = ctx
            sb, ps, own = self.sb, self.ps, self.sem
            w_hi = [sb(f"w_hi{s}", [128, KC, D], F32R) for s in range(S)]
            w_lo = [sb(f"w_lo{s}", [128, KC, D], F32R) for s in range(S)]
            w_raw = sb("w_raw", [128, 2, D], F32)
            self.inp = {n: sb(n, [P, b, src.shape[-1]], src.dtype) for n, src, _, b in self.inputs}
            x_hi = sb("x_hi", [128, 2, KC, P], F32R)
            x_lo = sb("x_lo", [128, 2, KC, P], F32R)
            self.out = {n: sb(n + "_o", [P, self.out_bufs, dst.shape[-1]], dt) for n, dst, _, dt in self.outputs}
            self.turned = turned = ps("turned", [128, 2, KC, 128], F32)
            self.acc = acc = ps("acc", [128, 2, D], F32)

            raw_in = [own("raw_in0"), own("raw_in1")]
            w_hi_made = own("w_hi_made")
            w_lo_made = own("w_lo_made")
            self.in_sem = {n: [own(f"{n}_in{b}") for b in range(bufs)] for n, _, _, bufs in self.inputs}
            self.out_sem = {n: [own(f"{n}_out{b}") for b in range(self.out_bufs)] for n, _, _, _ in self.outputs}
            self.prepared = [own(f"prepared{s}") for s in range(S)]
            self.transposed = transposed = own("transposed")
            x_hi_made = own("x_hi_made")
            x_lo_made = own("x_lo_made")
            self.multiplied = multiplied = own("multiplied")
            self.acc_read = own("acc_read")
            self.allocate()

            def buf(turn, s):
                return (turn.j * S + s) % 2

            def following(turn, s):
                if s + 1 < S:
                    return turn, s + 1
                known = turn.known()
                return (turn.after(1), 0) if known is None or known + 1 < NB else None

            with nc.Block() as block:
                @block.sync
                def _(sp):
                    def load(turn):
                        for name, src, first, bufs in self.inputs:
                            if turn.known() is None or turn.known() >= bufs:
                                self.input_free(sp, name, turn, bufs)
                            rows_dma(sp, self.inp[name][:, turn.slot(bufs), :], at(src, turn.row(plus=first)),
                                     self.in_sem[name][turn.slot(bufs)])

                    def store(turn):
                        for name, dst, first, dt in self.outputs:
                            self.output_ready(sp, name, turn)
                            tile = self.out[name][:, turn.slot(self.out_bufs), :]
                            rows_dma(sp, at(dst, turn.row(plus=first)), tile.bitcast(F32) if dt == F32R else tile,
                                     self.out_sem[name][turn.slot(self.out_bufs)])

                    load(Turn(0, 0, UNROLL))
                    self.before_sync(sp)
                    for n in range(S * KC):
                        s, c = divmod(n, KC)
                        if n >= 2:
                            sp.wait_ge(w_lo_made, n - 1)
                        sp.dma_start(w_raw[:, n % 2, :],
                                     self.weight(sp, s)[c * 128:(c + 1) * 128, :]).then_inc(raw_in[n % 2], 16)
                        if n == 1 and self.ahead == 2:
                            load(Turn(0, 1, UNROLL))

                    def tile(turn):
                        if turn.known() is None or turn.known() + self.ahead < NB:
                            load(turn.after(self.ahead))
                        store(turn)

                    all_tiles(sp, tile)
                    for name in self.out:
                        for b in range(self.out_bufs):
                            sp.wait_ge(self.out_sem[name][b], ROWS_SEM * len(range(b, NB, self.out_bufs)))

                @block.scalar
                def _(act):
                    self.before_scalar(act)
                    for n in range(S * KC):
                        s, c = divmod(n, KC)
                        act.wait_ge(raw_in[n % 2], 16 * (n // 2 + 1))
                        nc.scalar.activation(w_hi[s][:, c, :], w_raw[:, n % 2, :], ACT.Copy).then_inc(w_hi_made, 1)

                    def split(turn, s):
                        n, b = self.slots(turn, s), buf(turn, s)
                        act.wait_ge(transposed, n)
                        if not self.early(turn, s):
                            act.wait_ge(multiplied, n - 2)
                        nc.scalar.activation(x_hi[:, b, :, :], turned[:, b, :, 0:P], ACT.Copy).then_inc(x_hi_made, 1)

                    split(Turn(0, 0, UNROLL), 0)

                    def tile(turn):
                        for s in range(S):
                            if following(turn, s):
                                split(*following(turn, s))
                            self.finish_scalar(act, turn, s)

                    all_tiles(act, tile)

                @block.vector
                def _(dve):
                    self.before_vector(dve)
                    self.prepare_vector(dve, Turn(0, 0, UNROLL))
                    for n in range(S * KC):
                        s, c = divmod(n, KC)
                        dve.wait_ge(w_hi_made, n + 1)
                        nc.vector.tensor_tensor(w_lo[s][:, c, :], w_raw[:, n % 2, :], w_hi[s][:, c, :].bitcast(F32),
                                                ALU.subtract).then_inc(w_lo_made, 1)

                    def split(turn, s):
                        n, b = self.slots(turn, s), buf(turn, s)
                        dve.wait_ge(x_hi_made, n)
                        nc.vector.tensor_tensor(x_lo[:, b, :, :], turned[:, b, :, 0:P], x_hi[:, b, :, :].bitcast(F32),
                                                ALU.subtract).then_inc(x_lo_made, 1)

                    split(Turn(0, 0, UNROLL), 0)
                    if self.ahead == 2:
                        self.prepare_vector(dve, Turn(0, 1, UNROLL))

                    def tile(turn):
                        for s in range(S):
                            if following(turn, s):
                                split(*following(turn, s))
                            if s == 0 and (turn.known() is None or turn.known() + self.ahead < NB):
                                self.prepare_vector(dve, turn.after(self.ahead))
                            self.finish_vector(dve, turn, s)

                    all_tiles(dve, tile)
                    self.after_vector(dve)

                @block.gpsimd
                def _(pool):
                    all_tiles(pool, lambda turn: self.prepare_gpsimd(pool, turn))
                    self.after_gpsimd(pool)

                @block.tensor
                def _(pe):
                    def turn_over(turn, s):
                        n, b = self.slots(turn, s), buf(turn, s)
                        self.operand_ready(pe, turn, s)
                        if not self.early(turn, s):
                            pe.wait_ge(x_lo_made, n - 2)
                        for c in range(KC):
                            last = nc.tensor.transpose(turned[:, b, c, 0:P],
                                                       self.operand(turn, s)[:, c * 128:(c + 1) * 128],
                                                       self.ident[0:P, 0:P])
                        last.then_inc(transposed, 1)

                    def product(turn, s):
                        n, b = self.slots(turn, s), buf(turn, s)
                        pe.wait_ge(x_hi_made, n)
                        pe.wait_ge(x_lo_made, n)
                        if not self.early(turn, s):
                            pe.wait_ge(self.acc_read, n - 2)
                        for h in range(D // HALF):
                            cols = slice(h * HALF, (h + 1) * HALF)
                            for c in range(KC):
                                for m, (x, w) in enumerate(((x_hi, w_hi[s]), (x_hi, w_lo[s]), (x_lo, w_hi[s]))):
                                    last = nc.tensor.matmul(acc[0:P, b, cols], x[:, b, c, :], w[:, c, cols],
                                                            start=(c == 0 and m == 0), stop=(c == KC - 1 and m == 2))
                        last.then_inc(multiplied, 1)

                    turn_over(Turn(0, 0, UNROLL), 0)
                    pe.wait_ge(w_lo_made, KC * S)

                    def tile(turn):
                        for s in range(S):
                            if following(turn, s):
                                turn_over(*following(turn, s))
                            product(turn, s)

                    all_tiles(pe, tile)
                    self.after_tensor(pe)


class Norm:

    def __init__(self, stage, name):
        self.stage, self.nc, self.name = stage, stage.nc, name
        self.stats = stage.sb(name + "_stats", [P, 2, 2, 6], F32)
        self.moments = stage.sb(name + "_moments", [P, 2, 2], F32)
        self.var = stage.sb(name + "_var", [P, 2, 1], F32)
        self.rstd = stage.sb(name + "_rstd", [P, 2, 1], F32)
        self.minus_half = stage.sb(name + "_minus_half", [P, 1], F32)
        self.half_set = stage.sem(name + "_half_set")
        self.stats_made = stage.sem(name + "_stats_made")
        self.moments_made = stage.sem(name + "_moments_made")
        self.var_made = stage.sem(name + "_var_made")
        self.rstd_made = stage.sem(name + "_rstd_made")
        self.passed = stage.sem(name + "_passed")

    def set_constants(self):
        self.nc.vector.memset(self.minus_half[:, :], -0.5).then_inc(self.half_set, 1)

    def vector(self, dve, turn, out, free=None):
        nc, b, t = self.nc, turn.slot(2), turn.t(1)
        x = self.stage.inp[self.name][:, turn.slot(len(self.stage.in_sem[self.name])), :]
        self.stage.loaded(dve, self.name, turn)
        for h in range(D // HALF):
            last = nc.vector.bn_stats(self.stats[:, b, h, :], x[:, h * HALF:(h + 1) * HALF])
        last.then_inc(self.stats_made, 1)
        dve.wait_ge(self.stats_made, t)
        dve.sem_inc(self.passed, 1)
        nc.vector.bn_aggr(self.moments[:, b, :], self.stats[:, b, :, :]).then_inc(self.moments_made, 1)
        dve.wait_ge(self.moments_made, t)
        nc.vector.tensor_scalar(self.var[:, b, :], self.moments[:, b, 1:2], EPS, None, ALU.add).then_inc(self.var_made, 1)
        dve.wait_ge(self.rstd_made, t)
        if free:
            free(dve, turn)
        return nc.vector.tensor_scalar(out, x, self.moments[:, b, 0:1], self.rstd[:, b, :], ALU.subtract,
                                       ALU.mult)

    def gpsimd(self, pool, turn):
        if turn.known() == 0:
            pool.wait_ge(self.half_set, 1)
        pool.wait_ge(self.var_made, turn.t(1))
        self.nc.gpsimd.tensor_tensor(self.rstd[:, turn.slot(2), :], self.var[:, turn.slot(2), :], self.minus_half[:, :],
                                     ALU.pow).then_inc(self.rstd_made, 1)


class NormalisedDense(Dense):

    def allocate(self):
        self.norm = Norm(self, "x")
        self.xn = self.sb("xn", [P, 2, D], F32)

    def before_vector(self, dve):
        self.norm.set_constants()

    def xn_free(self, dve, turn):
        if turn.known() is None or turn.known() >= 2:
            dve.wait_ge(self.transposed, turn.t(-1))

    def prepare_vector(self, dve, turn):
        self.norm.vector(dve, turn, self.xn[:, turn.slot(2), :], self.xn_free).then_inc(self.prepared[0], 1)

    def prepare_gpsimd(self, pool, turn):
        self.norm.gpsimd(pool, turn)

    def operand(self, turn, s):
        return self.xn[:, turn.slot(2), :]

    def operand_ready(self, pe, turn, s):
        pe.wait_ge(self.prepared[0], turn.t(1))

    def input_free(self, sp, name, turn, bufs):
        sp.wait_ge(self.finished, turn.t(1 - bufs))


class GatProject(NormalisedDense):

    def __init__(self, nc, sem, ident, x, w, att_src, att_dst, xp, scores):
        super().__init__(nc, sem, ident, "gatp")
        self.weights = [w]
        self.inputs = [("x", x, 0, 4)]
        self.outputs = [("xp", xp, 0, F32), ("sc", scores, 0, F32)]
        self.att = (att_src, att_dst)

    def allocate(self):
        super().allocate()
        self.att_sb = self.sb("att", [P, 2, D], F32)
        self.junk = self.sb("junk", [P, 2, 2 * HEADS, C], BF16)
        self.att_in = self.sem("att_in")
        self.xp_made = self.acc_read
        self.finished = self.sem("finished")

    def before_sync(self, sp):
        for i in range(2):
            rows_dma(sp, self.att_sb[:, i, :], self.att[i].rearrange("h c -> (h c)").partition_broadcast(P), self.att_in)

    def finish_scalar(self, act, turn, s):
        b = turn.slot(2)
        act.wait_ge(self.multiplied, turn.t(1))
        self.output_free(act, "xp", turn)
        self.nc.scalar.activation(self.out["xp"][:, b, :], self.acc[0:P, b, :], ACT.Copy).then_inc(self.acc_read, 1)

    def finish_vector(self, dve, turn, s):
        nc, b = self.nc, turn.slot(2)
        if turn.known() == 0:
            dve.wait_ge(self.att_in, 2 * ROWS_SEM)
        dve.wait_ge(self.xp_made, turn.t(1))
        self.output_free(dve, "sc", turn)
        for i in range(2):
            for h in range(HEADS):
                last = nc.vector.tensor_tensor_reduce(out=self.junk[:, b, i * HEADS + h, :],
                                                      in0=self.out["xp"][:, b, h * C:(h + 1) * C],
                                                      in1=self.att_sb[:, i, h * C:(h + 1) * C], scale=1.0, scalar=0.0,
                                                      op0=ALU.mult, op1=ALU.add,
                                                      accum_out=self.out["sc"][:, b, i * HEADS + h:i * HEADS + h + 1])
        last.then_inc(self.finished, 1)

    def output_ready(self, sp, name, turn):
        sp.wait_ge(self.finished, turn.t(1))


CHUNKS = [4, 3, 3, 3, 3, 3, 3, 3]
START = [sum(CHUNKS[:c]) for c in range(len(CHUNKS) + 1)]
NC = len(CHUNKS)
BUFS = 4
LEAD = 3
PIECES = [(0, START[3]), (START[3], START[6]), (START[6], NB)]
PIECE_OF = [0, 0, 0, 1, 1, 1, 2, 2]
GROUPS = HEADS // 2
GW = 2 * C
SEEN = 3


class Block2:

    def __init__(self, g, i, k):
        self.g, self.i, self.k = g, i + k // 2 if k >= 2 else i, k % 2

    def next(self):
        return Block2(self.g, self.i, self.k + 1)

    def blocks(self):
        return self.g * NB + (self.i * 2 + (self.k + 1))

    def slots(self, j):
        return self.g * (2 * NB) + (self.i * 4 + (2 * self.k + j + 1))

    def chunks(self, j, c):
        return self.g * (2 * NB * NC) + (self.i * (4 * NC) + ((2 * self.k + j) * NC + c + 1))

    def use(self):
        return self.g * ((NB + 1) // 2 if self.k == 0 else NB // 2) + (self.i + 1)

    def index(self, scale, plus=0):
        return self.i * (2 * scale) + (self.k * scale + plus)


def passes(eng, number, start, body):
    with eng.Fori(0, number) as g:
        start(g)
        with eng.Fori(0, (NB - SEEN) // 2) as i:
            for k in range(2):
                body(Block2(g, i, k), SEEN)
        for left in reversed(range(SEEN)):
            b = NB - 1 - left
            body(Block2(g, b // 2, b % 2), left)


def attend(nc, sem, ident, x, xp, scores, score_rows, counts, bias, x1):
    with ExitStack() as ctx:
        def sb(name, shape, dt):
            return ctx.enter_context(nc.sbuf_tensor("att_" + name, shape, dt))

        def own(name):
            return sem("att_" + name)

        xp_sb = sb("xp", [P, NB, 2, C + 1], F32)
        srow = sb("srow", [P, 2, NODES], F32)
        cnt = sb("cnt", [P, NODES], U16)
        cnt_f = sb("cnt_f", [P, NODES], F32)
        gone = sb("gone", [P, NODES], BF16)
        wt = sb("wt", [P, 4, NODES], F32)
        flipped = sb("flipped", [P, BUFS, max(CHUNKS), P], F32)
        cols = sb("cols", [P, NB * 2 * HEADS], F32)
        bias_sb = sb("bias", [P, 2, C], F32)
        xin = sb("xin", [P, GW], F32)
        sums = sb("sums", [P, 2, C], F32)
        x1_sb = sb("x1", [P, GW], F32)
        a_dst = sb("a_dst", [P, 2, 2], F32)
        top = sb("top", [P, 2, 2], F32)
        raised = sb("raised", [P, 2, 2], F32)
        minus = sb("minus", [P, 2, 2], F32)
        shift = sb("shift", [P, 2, 2], F32)
        inv = sb("inv", [P, 2, 1], F32)
        picked = sb("picked", [P, HEADS, NB], F32)
        rows_sb = sb("rows", [NB, HEADS, P], F32)
        turned = ctx.enter_context(nc.psum_tensor("att_turned", [128, BUFS, 4, 128], F32))
        acc = ctx.enter_context(nc.psum_tensor("att_acc", [128, 2, 512], F32))

        cols_in = own("cols_in")
        picked_made = own("picked_made")
        rows_turned = own("rows_turned")
        rows_made = own("rows_made")
        rows_out = own("rows_out")
        set_up = own("set_up")
        zero_out = own("zero_out")
        group_in = own("group_in")
        cnt_in = own("cnt_in")
        x_in = own("x_in")
        x1_out = own("x1_out")
        counts_cast = own("counts_cast")
        held = own("held")
        passed = own("passed")
        cast_may_start = own("cast_may_start")
        a_dst_made = own("a_dst_made")
        gone_made = own("gone_made")
        top_made = own("top_made")
        raised_made = own("raised_made")
        minus_made = own("minus_made")
        shift_made = own("shift_made")
        scores_made = own("scores_made")
        leaky_made = own("leaky_made")
        exp_made = own("exp_made")
        weighted = own("weighted")
        chunk_turned = own("chunk_turned")
        chunk_flipped = own("chunk_flipped")
        chunk_done = own("chunk_done")
        inv_made = own("inv_made")
        sums_made = own("sums_made")
        finished = own("finished")
        counts2 = counts[0:NODES * NODES, :].rearrange("(d s) o -> d (s o)", s=NODES)

        with nc.Block() as block:
            @block.sync
            def _(sp):
                rows_dma(sp, cols[:, :].rearrange("p (b h) -> p b h", b=NB), scores.rearrange("(b p) h -> p b h", p=P),
                         cols_in)
                sp.wait_ge(set_up, 1)
                for h in range(2):
                    sp.dma_start(x1[0:1, h * GW:(h + 1) * GW].rearrange("o (k f) -> o k f", k=2), sums[0:1, :, :]
                                 ).then_inc(zero_out, 16)
                sp.wait_ge(rows_made, 1)
                sp.dma_start(score_rows.rearrange("h (b p) -> b h p", p=P), rows_sb[:, :, :]).then_inc(rows_out, 16)
                sp.wait_ge(rows_out, 16)
                sp.sem_inc(x1_out, ROWS_SEM)

                def load_counts(blk):
                    hold(sp, held, gone_made, blk.blocks())
                    hold(sp, held, counts_cast, blk.blocks())
                    rows_dma(sp, cnt[:, :], counts2[bass.ds(blk.index(P), P)], cnt_in)

                def load_x(blk):
                    hold(sp, held, finished, blk.blocks() * 2)
                    rows_dma(sp, xin[:, :], x[bass.ds(blk.index(P), P), bass.ds(blk.g * GW, GW)], x_in)

                def start(g):
                    hold(sp, held, finished, g * (2 * NB) + 2)
                    rows_dma(sp, srow[:, :, :], score_rows[bass.ds(g * 2, 2)].partition_broadcast(P), group_in)
                    rows_dma(sp, bias_sb[:, :, :], bias[bass.ds(g * GW, GW)].rearrange("(h c) -> h c", h=2)
                             .partition_broadcast(P), group_in)
                    load_counts(Block2(g, 0, 0))
                    for j in range(2):
                        rows_dma(sp, xp_sb[:, :, j, 0:C],
                                 xp.rearrange("(b p) f -> p b f", p=P)[:, :, bass.ds(g * GW + j * C, C)], group_in)
                    load_x(Block2(g, 0, 0))
                    load_counts(Block2(g, 0, 1))

                def body(blk, left):
                    if left >= 2:
                        load_counts(blk.next().next())
                    hold(sp, held, finished, blk.slots(1) + 2)
                    rows_dma(sp, x1[bass.ds(blk.index(P, 1), P), bass.ds(blk.g * GW, GW)], x1_sb[:, :], x1_out)
                    if left >= 1:
                        load_x(blk.next())

                passes(sp, GROUPS, start, body)
                sp.wait_ge(zero_out, 32)
                sp.wait_ge(x1_out, ROWS_SEM * (1 + GROUPS * NB))

            @block.vector
            def _(dve):
                nc.vector.memset(sums[0:1, :, :], 0.0).then_inc(set_up, 1)
                dve.wait_ge(cols_in, ROWS_SEM)
                nc.vector.tensor_copy(picked[:, :, :], cols[:, :].rearrange("p (b h) -> p h b", b=NB)[:, 0:HEADS, :]
                                      ).then_inc(picked_made, 1)
                nc.vector.memset(xp_sb[:, :, :, C:C + 1], 1.0).then_inc(set_up, 1)
                dve.wait_ge(rows_turned, 1)
                nc.vector.tensor_copy(rows_sb[:, :, :], turned[0:NB, 0, :, 0:P]).then_inc(rows_made, 1)
                for s, credit in ((finished, 2), (gone_made, 1), (top_made, 1)):
                    dve.sem_inc(s, credit)
                dve.wait_ge(zero_out, 32)

                def bar(blk):
                    nc.vector.tensor_copy(a_dst[:, blk.k, :], cols[:, bass.ds(blk.index(2 * HEADS, HEADS) + blk.g * 2, 2)]
                                          ).then_inc(a_dst_made, 1)
                    dve.wait_ge(cnt_in, blk.blocks() * ROWS_SEM)
                    dve.wait_ge(top_made, blk.slots(0))
                    nc.vector.tensor_scalar(gone[:, :], cnt[:, :], 0.0, MASKED, ALU.is_equal, ALU.mult
                                            ).then_inc(gone_made, 1)

                def maximum(blk, j):
                    n, k = blk.slots(j), blk.k
                    dve.wait_ge(chunk_turned, n * NC)
                    dve.wait_ge(gone_made, blk.blocks() + 1)
                    dve.sem_inc(passed, 1)
                    nc.vector.tensor_tensor_reduce(out=wt[:, 2 * k + j, :], in0=srow[:, j, :], in1=gone[:, :], scale=1.0,
                                                   scalar=-3.4e38, op0=ALU.add, op1=ALU.max,
                                                   accum_out=top[:, k, j:j + 1]).then_inc(top_made, 1)
                    dve.wait_ge(top_made, n + 1)
                    dve.wait_ge(a_dst_made, blk.blocks())
                    nc.vector.tensor_tensor(raised[:, k, j:j + 1], top[:, k, j:j + 1], a_dst[:, k, j:j + 1], ALU.add
                                            ).then_inc(raised_made, 1)
                    dve.wait_ge(raised_made, n)
                    nc.vector.tensor_scalar(minus[:, k, j:j + 1], raised[:, k, j:j + 1], -1.0, None, ALU.mult
                                            ).then_inc(minus_made, 1)
                    dve.wait_ge(minus_made, n)
                    nc.vector.scalar_tensor_tensor(out=shift[:, k, j:j + 1], in0=raised[:, k, j:j + 1], scalar=-SLOPE,
                                                   in1=minus[:, k, j:j + 1], op0=ALU.mult, op1=ALU.min
                                                   ).then_inc(shift_made, 1)

                def leaky(blk, j):
                    w = wt[:, 2 * blk.k + j, :]
                    dve.wait_ge(scores_made, blk.slots(j))
                    nc.vector.scalar_tensor_tensor(out=w, in0=w, scalar=SLOPE, in1=w, op0=ALU.mult, op1=ALU.max
                                                   ).then_inc(leaky_made, 1)

                def finish(blk, j):
                    n, span = blk.slots(j), slice(j * C, (j + 1) * C)
                    dve.wait_ge(chunk_done, blk.chunks(j, NC - 1) + BUFS)
                    nc.vector.reciprocal(inv[:, j, :], acc[0:P, j, C:C + 1]).then_inc(inv_made, 1)
                    dve.wait_ge(inv_made, n)
                    nc.vector.scalar_tensor_tensor(out=sums[:, j, :], in0=acc[0:P, j, 0:C], scalar=inv[:, j, :],
                                                   in1=bias_sb[:, j, :], op0=ALU.mult, op1=ALU.add).then_inc(sums_made, 1)
                    dve.wait_ge(x_in, blk.blocks() * ROWS_SEM)
                    dve.wait_ge(x1_out, blk.blocks() * ROWS_SEM)
                    dve.wait_ge(sums_made, n)
                    nc.vector.scalar_tensor_tensor(out=x1_sb[:, span], in0=sums[:, j, :], scalar=0.0,
                                                   in1=xin[:, span], op0=ALU.max, op1=ALU.add).then_inc(finished, 1)

                def start(g):
                    first = Block2(g, 0, 0)
                    dve.wait_ge(group_in, (g + 1) * (4 * ROWS_SEM))
                    bar(first)
                    maximum(first, 0)
                    maximum(first, 1)
                    leaky(first, 0)
                    leaky(first, 1)
                    bar(first.next())
                    maximum(first.next(), 0)

                def body(blk, left):
                    if left >= 1:
                        leaky(blk.next(), 0)
                        maximum(blk.next(), 1)
                    finish(blk, 0)
                    if left >= 1:
                        leaky(blk.next(), 1)
                    if left >= 2:
                        bar(blk.next().next())
                        maximum(blk.next().next(), 0)
                    finish(blk, 1)

                passes(dve, GROUPS, start, body)

            @block.scalar
            def _(act):
                act.sem_inc(chunk_flipped, BUFS)

                def add_dst(blk, j):
                    w = wt[:, 2 * blk.k + j, :]
                    act.wait_ge(top_made, blk.slots(j) + 1)
                    act.wait_ge(a_dst_made, blk.blocks())
                    nc.scalar.activation(w, w, ACT.Identity, bias=a_dst[:, blk.k, j:j + 1]).then_inc(scores_made, 1)

                def exp(blk, j):
                    w = wt[:, 2 * blk.k + j, :]
                    act.wait_ge(leaky_made, blk.slots(j))
                    act.wait_ge(shift_made, blk.slots(j))
                    nc.scalar.activation(w, w, ACT.Exp, bias=shift[:, blk.k, j:j + 1]).then_inc(exp_made, 1)

                def flip(blk, j, c):
                    n = blk.chunks(j, c)
                    act.wait_ge(chunk_turned, n + 4 * NC)
                    act.wait_ge(chunk_done, n)
                    nc.scalar.activation(flipped[:, c % BUFS, 0:CHUNKS[c], :], turned[0:P, c % BUFS, 0:CHUNKS[c], 0:P],
                                         ACT.Copy).then_inc(chunk_flipped, 1)

                def start(g):
                    first = Block2(g, 0, 0)
                    act.wait_ge(group_in, (g + 1) * (4 * ROWS_SEM))
                    add_dst(first, 0)
                    add_dst(first, 1)
                    exp(first, 0)
                    exp(first, 1)
                    add_dst(first.next(), 0)

                def body(blk, left):
                    for j in range(2):
                        for c in range(NC):
                            flip(blk, j, c)
                            if c == 2 and left >= 1:
                                exp(blk.next(), j)
                            if c == 5 and j == 0 and left >= 1:
                                add_dst(blk.next(), 1)
                            if c == 5 and j == 1 and left >= 2:
                                add_dst(blk.next().next(), 0)

                passes(act, GROUPS, start, body)

            @block.gpsimd
            def _(pool):
                pool.sem_inc(counts_cast, 1)
                pool.sem_inc(weighted, 1)

                def cast(blk):
                    pool.wait_ge(cnt_in, blk.blocks() * ROWS_SEM)
                    pool.sem_inc(cast_may_start, 1)
                    pool.wait_ge(weighted, blk.slots(0) * 3 - 2)
                    pool.sem_inc(cast_may_start, 1)
                    nc.gpsimd.tensor_copy(cnt_f[:, :], cnt[:, :]).then_inc(counts_cast, 1)

                def weigh(blk, j):
                    pool.wait_ge(exp_made, blk.slots(j))
                    pool.wait_ge(counts_cast, blk.blocks() + 1)
                    for b0, b1 in PIECES:
                        w = wt[:, 2 * blk.k + j, b0 * P:b1 * P]
                        nc.gpsimd.tensor_tensor(w, w, cnt_f[:, b0 * P:b1 * P], ALU.mult).then_inc(weighted, 1)

                def body(blk, left):
                    cast(blk)
                    weigh(blk, 0)
                    weigh(blk, 1)

                passes(pool, GROUPS, lambda g: None, body)

            @block.tensor
            def _(pe):
                pe.wait_ge(picked_made, 1)
                for h in range(HEADS):
                    last_t = nc.tensor.transpose(turned[0:NB, 0, h, 0:P], picked[:, h, :], ident[0:P, 0:P])
                last_t.then_inc(rows_turned, 1)
                pe.wait_ge(rows_made, 1)
                pe.wait_ge(set_up, 2)
                pe.sem_inc(chunk_turned, 4 * NC)
                pe.sem_inc(chunk_done, BUFS)

                def turn_over(blk, j, c):
                    n = blk.chunks(j, c)
                    pe.wait_ge(weighted, (blk.slots(j) - 1) * 3 + (PIECE_OF[c] + 2))
                    pe.wait_ge(chunk_flipped, n)
                    for b in range(CHUNKS[c]):
                        last = nc.tensor.transpose(turned[0:P, c % BUFS, b, 0:P],
                                                   wt[:, 2 * blk.k + j, (START[c] + b) * P:(START[c] + b + 1) * P],
                                                   ident[0:P, 0:P])
                    last.then_inc(chunk_turned, 1)

                def product(blk, j, c):
                    pe.wait_ge(chunk_flipped, blk.chunks(j, c) + BUFS)
                    if c == 0:
                        pe.wait_ge(finished, blk.slots(j))
                    for b in range(CHUNKS[c]):
                        last = nc.tensor.matmul(acc[0:P, j, 0:C + 1], flipped[:, c % BUFS, b, :], xp_sb[:, START[c] + b, j, :],
                                                start=(c == 0 and b == 0), stop=(c == NC - 1 and b == CHUNKS[c] - 1))
                    last.then_inc(chunk_done, 1)

                def start(g):
                    hold(pe, held, group_in, (g + 1) * (4 * ROWS_SEM))
                    for c in range(LEAD):
                        turn_over(Block2(g, 0, 0), 0, c)

                def body(blk, left):
                    for j in range(2):
                        for c in range(NC):
                            if c + LEAD < NC:
                                turn_over(blk, j, c + LEAD)
                            elif j == 0:
                                turn_over(blk, 1, c + LEAD - NC)
                            elif left >= 1:
                                turn_over(blk.next(), 0, c + LEAD - NC)
                            product(blk, j, c)

                passes(pe, GROUPS, start, body)


class Mix(Dense):
    ahead, out_bufs = 1, 1

    def __init__(self, nc, sem, ident, x1, wr, wk, mu_r, mu_k, r, k):
        super().__init__(nc, sem, ident, "mix")
        self.weights = [wr, wk]
        self.inputs = [("x", x1, 1, 2), ("prev", x1, 0, 2)]
        self.outputs = [("r", r, 0, F32), ("k", k, 0, F32)]
        self.mu = (mu_r, mu_k)

    def allocate(self):
        self.norm = Norm(self, "x")
        self.norm_prev = Norm(self, "prev")
        self.mu_sb = self.sb("mu", [P, 2, D], F32)
        self.rest = self.sb("rest", [P, D], F32)
        self.mixed = self.sb("mixed", [P, 2, D], F32)
        self.part = self.sb("part", [P, 2, D], F32)
        self.mu_in = self.sem("mu_in")
        self.rest_made = self.sem("rest_made")
        self.normed = self.sem("normed")
        self.part_made = [self.sem("part_made0"), self.sem("part_made1")]
        self.main_made = [self.sem("main_made0"), self.sem("main_made1")]
        self.relu_made = self.sem("relu_made")
        self.k_made = self.sem("k_made")

    def before_sync(self, sp):
        for i in range(2):
            rows_dma(sp, self.mu_sb[:, i, :], self.mu[i].partition_broadcast(P), self.mu_in)

    def before_vector(self, dve):
        self.norm.set_constants()
        self.norm_prev.set_constants()
        dve.wait_ge(self.mu_in, 2 * ROWS_SEM)
        self.nc.vector.tensor_scalar(self.rest[:, :], self.mu_sb[:, 1, :], -1.0, 1.0, ALU.mult, ALU.add
                                     ).then_inc(self.rest_made, 1)

    def prepare_vector(self, dve, turn):
        nc, b, t = self.nc, turn.slot(2), turn.t(1)
        x, prev = self.inp["x"][:, b, :], self.inp["prev"][:, b, :]
        self.norm.vector(dve, turn, x).then_inc(self.normed, 1)
        self.norm_prev.vector(dve, turn, prev).then_inc(self.normed, 1)
        dve.wait_ge(self.normed, t * 2)
        if turn.known() is None or turn.known() >= 1:
            dve.wait_ge(self.transposed, t * 2 - 3)
        nc.vector.tensor_tensor(self.mixed[:, 0, :], x, self.mu_sb[:, 0, :], ALU.mult).then_inc(self.main_made[0], 1)
        nc.vector.scalar_tensor_tensor(out=self.part[:, 0, :], in0=self.mu_sb[:, 0, :], scalar=-1.0, in1=prev,
                                       op0=ALU.add, op1=ALU.mult).then_inc(self.part_made[0], 1)
        dve.wait_ge(self.main_made[0], t)
        dve.wait_ge(self.part_made[0], t)
        nc.vector.tensor_tensor(self.mixed[:, 0, :], self.mixed[:, 0, :], self.part[:, 0, :], ALU.subtract
                                ).then_inc(self.prepared[0], 1)

    def prepare_gpsimd(self, pool, turn):
        nc, b, t = self.nc, turn.slot(2), turn.t(1)
        x, prev = self.inp["x"][:, b, :], self.inp["prev"][:, b, :]
        self.norm.gpsimd(pool, turn)
        self.norm_prev.gpsimd(pool, turn)
        if turn.known() == 0:
            pool.wait_ge(self.rest_made, 1)
        pool.wait_ge(self.normed, t * 2)
        if turn.known() is None or turn.known() >= 1:
            pool.wait_ge(self.transposed, t * 2 - 2)
        nc.gpsimd.tensor_tensor(self.mixed[:, 1, :], x, self.mu_sb[:, 1, :], ALU.mult).then_inc(self.main_made[1], 1)
        nc.gpsimd.tensor_tensor(self.part[:, 1, :], prev, self.rest[:, :], ALU.mult).then_inc(self.part_made[1], 1)
        pool.wait_ge(self.main_made[1], t)
        pool.wait_ge(self.part_made[1], t)
        nc.gpsimd.tensor_tensor(self.mixed[:, 1, :], self.mixed[:, 1, :], self.part[:, 1, :], ALU.add
                                ).then_inc(self.prepared[1], 1)

    def operand(self, turn, s):
        return self.mixed[:, s, :]

    def operand_ready(self, pe, turn, s):
        pe.wait_ge(self.prepared[s], turn.t(1))

    def input_free(self, sp, name, turn, bufs):
        for s in range(2):
            sp.wait_ge(self.prepared[s], turn.t(1 - bufs))

    def finish_scalar(self, act, turn, s):
        nc, b = self.nc, (turn.j * 2 + s) % 2
        name = "rk"[s]
        act.wait_ge(self.multiplied, self.slots(turn, s))
        self.output_free(act, name, turn)
        if s == 0:
            nc.scalar.activation(self.out["r"][:, 0, :], self.acc[0:P, b, :], ACT.Sigmoid).then_inc(self.acc_read, 1)
        else:
            nc.scalar.activation(self.out["k"][:, 0, :], self.acc[0:P, b, :], ACT.Relu).then_inc(self.acc_read, 1)
            act.wait_ge(self.acc_read, self.slots(turn, s))
            nc.scalar.activation(self.out["k"][:, 0, :], self.out["k"][:, 0, :], ACT.Square).then_inc(self.k_made, 1)

    def output_ready(self, sp, name, turn):
        if name == "r":
            sp.wait_ge(self.acc_read, self.slots(turn, 0))
        else:
            sp.wait_ge(self.k_made, turn.t(1))


class Value(Dense):

    def __init__(self, nc, sem, ident, k, r, x1, wv, counts, x2, dinv):
        super().__init__(nc, sem, ident, "val")
        self.weights = [wv]
        self.inputs = [("k", k, 0, 2), ("cnt", counts, 0, 2), ("r", r, 0, 4), ("x", x1, 1, 4)]
        self.outputs = [("x2", x2, 0, F32)]
        self.dinv = dinv

    def allocate(self):
        self.gated = self.sb("gated", [P, 2, D], F32)
        self.total = self.sb("total", [P, NODES], F32)
        self.ones = self.sb("ones", [P, 2], F32)
        self.degree = self.sb("degree", [P, NB], F32)
        self.half = self.sb("half", [P, NB], F32)
        self.consts_set = self.sem("consts_set")
        self.total_made = self.sem("total_made")
        self.finished = self.sem("finished")
        self.summed = self.sem("summed")
        self.degree_made = self.sem("degree_made")
        self.dinv_made = self.sem("dinv_made")
        self.degrees = self.ps_turned_view

    def ps_turned_view(self):
        return self.turned[0:P, 0, 0, 0:2 * NB].rearrange("p (b o) -> p b o", o=2)

    def before_vector(self, dve):
        self.nc.vector.memset(self.total[:, :], 0.0).then_inc(self.total_made, 1)
        self.nc.vector.memset(self.ones[:, :], 1.0).then_inc(self.consts_set, 1)
        self.nc.vector.memset(self.half[:, :], -0.5).then_inc(self.consts_set, 1)

    def operand(self, turn, s):
        return self.inp["k"][:, turn.slot(2), :]

    def operand_ready(self, pe, turn, s):
        self.loaded(pe, "k", turn)

    def input_free(self, sp, name, turn, bufs):
        if name == "k":
            sp.wait_ge(self.transposed, turn.t(1 - bufs))
        elif name == "cnt":
            sp.wait_ge(self.total_made, turn.t(1 - bufs) + 1)
        else:
            sp.wait_ge(self.finished, turn.t(1 - bufs))

    def finish_vector(self, dve, turn, s):
        nc, b, t = self.nc, turn.slot(2), turn.t(1)
        self.loaded(dve, "cnt", turn)
        dve.wait_ge(self.total_made, t)
        nc.vector.tensor_tensor(self.total[:, :], self.total[:, :], self.inp["cnt"][:, b, :], ALU.add
                                ).then_inc(self.total_made, 1)
        dve.wait_ge(self.multiplied, t)
        self.loaded(dve, "r", turn)
        nc.vector.tensor_tensor(self.gated[:, b, :], self.acc[0:P, b, :], self.inp["r"][:, turn.slot(4), :], ALU.mult
                                ).then_inc(self.acc_read, 1)
        self.loaded(dve, "x", turn)
        self.output_free(dve, "x2", turn)
        dve.wait_ge(self.acc_read, t)
        nc.vector.tensor_tensor(self.out["x2"][:, b, :], self.gated[:, b, :], self.inp["x"][:, turn.slot(4), :], ALU.add
                                ).then_inc(self.finished, 1)

    def output_ready(self, sp, name, turn):
        sp.wait_ge(self.finished, turn.t(1))

    def after_tensor(self, pe):
        pe.wait_ge(self.total_made, NB + 1)
        pe.wait_ge(self.consts_set, 2)
        for b in range(NB):
            last = self.nc.tensor.matmul(self.degrees()[:, b, :], self.total[:, b * P:(b + 1) * P], self.ones[:, :],
                                         start=True, stop=True)
        last.then_inc(self.summed, 1)

    def after_vector(self, dve):
        dve.wait_ge(self.summed, 1)
        self.nc.vector.tensor_copy(self.degree[:, :], self.degrees()[:, :, 0]).then_inc(self.degree_made, 1)

    def after_gpsimd(self, pool):
        pool.wait_ge(self.degree_made, 1)
        self.nc.gpsimd.tensor_tensor(self.dinv[:, :], self.degree[:, :], self.half[:, :], ALU.pow
                                     ).then_inc(self.dinv_made, 1)
        pool.wait_ge(self.dinv_made, 1)


class GcnProject(NormalisedDense):

    def __init__(self, nc, sem, ident, x2, w, b, dinv, h_hi, h_lo):
        super().__init__(nc, sem, ident, "gcnp")
        self.weights = [w]
        self.inputs = [("x", x2, 0, 4)]
        self.outputs = [("hi", h_hi, 0, F32R), ("lo", h_lo, 0, F32R)]
        self.b, self.dinv = b, dinv

    def allocate(self):
        super().allocate()
        self.b_sb = self.sb("b", [P, D], F32)
        self.sums = self.sb("sums", [P, 2, D], F32)
        self.scale = self.sb("scale", [P, 2, 1], F32)
        self.b_in = self.sem("b_in")
        self.scale_made = self.sem("scale_made")
        self.hi_made = self.sem("hi_made")
        self.finished = self.sem("finished")

    def before_sync(self, sp):
        rows_dma(sp, self.b_sb[:, :], self.b.partition_broadcast(P), self.b_in)

    def finish_vector(self, dve, turn, s):
        nc, b, t = self.nc, turn.slot(2), turn.t(1)
        nc.vector.tensor_copy(self.scale[:, b, :], self.dinv[:, bass.ds(turn.t(), 1)]).then_inc(self.scale_made, 1)
        if turn.known() == 0:
            dve.wait_ge(self.b_in, ROWS_SEM)
        dve.wait_ge(self.multiplied, t)
        nc.vector.tensor_tensor(self.sums[:, b, :], self.acc[0:P, b, :], self.b_sb[:, :], ALU.add
                                ).then_inc(self.acc_read, 1)
        self.output_free(dve, "lo", turn)
        dve.wait_ge(self.hi_made, t)
        nc.vector.scalar_tensor_tensor(out=self.out["lo"][:, b, :], in0=self.sums[:, b, :], scalar=self.scale[:, b, :],
                                       in1=self.out["hi"][:, b, :].bitcast(F32), op0=ALU.mult, op1=ALU.subtract
                                       ).then_inc(self.finished, 1)

    def finish_scalar(self, act, turn, s):
        b, t = turn.slot(2), turn.t(1)
        act.wait_ge(self.acc_read, t)
        act.wait_ge(self.scale_made, t)
        self.output_free(act, "hi", turn)
        self.nc.scalar.activation(self.out["hi"][:, b, :], self.sums[:, b, :], ACT.Copy, scale=self.scale[:, b, :]
                                  ).then_inc(self.hi_made, 1)

    def output_ready(self, sp, name, turn):
        sp.wait_ge(self.finished, turn.t(1))


def propagate(nc, sem, h_hi, h_lo, counts, dinv, x2, x3):
    with ExitStack() as ctx:
        def sb(name, shape, dt):
            return ctx.enter_context(nc.sbuf_tensor("prop_" + name, shape, dt))

        def own(name):
            return sem("prop_" + name)

        hh = sb("hh", [P, NB, HALF], F32R)
        hl = sb("hl", [P, NB, HALF], F32R)
        cnt = sb("cnt", [P, 2, NB, P], U16)
        c_hi = sb("c_hi", [P, 2, NB, P], F32R)
        c_lo = sb("c_lo", [P, 2, NB, P], F32R)
        xin = sb("xin", [P, 2, HALF], F32)
        x3_sb = sb("x3", [P, 2, HALF], F32)
        scale = sb("scale", [P, 2, 1], F32)
        acc = ctx.enter_context(nc.psum_tensor("prop_acc", [128, 2, HALF], F32))
        half_in = own("half_in")
        held = own("held")
        cnt_in = [own("cnt_in0"), own("cnt_in1")]
        x_in = [own("x_in0"), own("x_in1")]
        x3_out = [own("x3_out0"), own("x3_out1")]
        hi_made = own("hi_made")
        lo_made = own("lo_made")
        scale_made = own("scale_made")
        multiplied = own("multiplied")
        finished = own("finished")
        counts3 = counts[0:NODES * NODES, :].rearrange("(b p s) o -> p b (s o)", p=P, s=NODES)

        with nc.Block() as block:
            @block.sync
            def _(sp):
                for b in range(2):
                    sp.sem_inc(x3_out[b], ROWS_SEM)

                def load_block(blk):
                    n = blk.blocks()
                    hold(sp, held, lo_made, n)
                    rows_dma(sp, cnt[:, blk.k, :, :], counts3[:, :, bass.ds(blk.index(P), P)], cnt_in[blk.k])
                    hold(sp, held, finished, n)
                    rows_dma(sp, xin[:, blk.k, :], x2[bass.ds(blk.index(P), P), bass.ds(blk.g * HALF, HALF)], x_in[blk.k])

                def start(g):
                    hold(sp, held, finished, g * NB + 2)
                    load_block(Block2(g, 0, 0))
                    for dst, src in ((hh, h_hi), (hl, h_lo)):
                        rows_dma(sp, dst[:, :, :].bitcast(F32),
                                 src.rearrange("(b p) f -> p b f", p=P)[:, :, bass.ds(g * HALF, HALF)], half_in)

                def body(blk, left):
                    if left >= 1:
                        load_block(blk.next())
                    hold(sp, held, finished, blk.blocks() + 2)
                    rows_dma(sp, x3[bass.ds(blk.index(P), P), bass.ds(blk.g * HALF, HALF)], x3_sb[:, blk.k, :],
                             x3_out[blk.k])

                passes(sp, 2, start, body)
                for b in range(2):
                    sp.wait_ge(x3_out[b], ROWS_SEM * (1 + 2 * ((NB + 1 - b) // 2)))

            @block.scalar
            def _(act):
                def split(blk):
                    act.wait_ge(cnt_in[blk.k], blk.use() * ROWS_SEM)
                    act.wait_ge(multiplied, blk.blocks())
                    nc.scalar.activation(c_hi[:, blk.k, :, :], cnt[:, blk.k, :, :], ACT.Copy).then_inc(hi_made, 1)

                passes(act, 2, lambda g: None, lambda blk, left: split(blk))

            @block.vector
            def _(dve):
                for s in (lo_made, finished):
                    dve.sem_inc(s, 2)

                def split(blk):
                    dve.wait_ge(hi_made, blk.blocks())
                    nc.vector.tensor_tensor(c_lo[:, blk.k, :, :], cnt[:, blk.k, :, :], c_hi[:, blk.k, :, :].bitcast(F32),
                                            ALU.subtract).then_inc(lo_made, 1)

                def finish(blk):
                    k = blk.k
                    nc.vector.tensor_copy(scale[:, k, :], dinv[:, bass.ds(blk.index(1), 1)]).then_inc(scale_made, 1)
                    dve.wait_ge(multiplied, blk.blocks() + 2)
                    dve.wait_ge(x_in[k], blk.use() * ROWS_SEM)
                    dve.wait_ge(x3_out[k], blk.use() * ROWS_SEM)
                    dve.wait_ge(scale_made, blk.blocks())
                    nc.vector.scalar_tensor_tensor(out=x3_sb[:, k, :], in0=acc[0:P, k, :], scalar=scale[:, k, :],
                                                   in1=xin[:, k, :], op0=ALU.mult, op1=ALU.add).then_inc(finished, 1)

                def body(blk, left):
                    if left >= 1:
                        split(blk.next())
                    finish(blk)

                passes(dve, 2, lambda g: split(Block2(g, 0, 0)), body)

            @block.tensor
            def _(pe):
                pe.sem_inc(multiplied, 2)

                def body(blk, left):
                    pe.wait_ge(lo_made, blk.blocks() + 2)
                    pe.wait_ge(finished, blk.blocks())
                    for b in range(NB):
                        for m, (c, h) in enumerate(((c_hi, hh), (c_lo, hh), (c_hi, hl))):
                            done = nc.tensor.matmul(acc[0:P, blk.k, :], c[:, blk.k, b, :], h[:, b, :],
                                                    start=(b == 0 and m == 0), stop=(b == NB - 1 and m == 2))
                    done.then_inc(multiplied, 1)

                passes(pe, 2, lambda g: hold(pe, held, half_in, (g + 1) * (2 * ROWS_SEM)), body)


class Expert(NormalisedDense):

    def __init__(self, nc, sem, ident, x3, w, b, logits, u, out):
        super().__init__(nc, sem, ident, "exp")
        self.weights = [w]
        self.inputs = [("x", x3, 0, 4)]
        self.outputs = [("y", out, 0, F32)]
        self.b, self.logits, self.u = b, logits, u
        self.experts = w.shape[0]

    def allocate(self):
        super().allocate()
        E = self.experts
        self.b_sb = self.sb("b", [P, D], F32)
        self.sums = self.sb("sums", [P, 2, D], F32)
        self.given = self.sb("given", [1, 2, E], F32)
        self.logs = self.sb("logs", [1, 2, E], F32)
        self.small = self.sb("small", [1, 4], F32)
        self.expo = self.sb("expo", [1, E], F32)
        self.score = self.sb("score", [1, 2, E], F32)
        self.best = self.sb("best", [1, 8], F32)
        self.index = self.sb("index", [1, 8], U32)
        self.given_in = self.sem("given_in")
        self.b_in = self.sem("b_in")
        self.log_made = self.sem("log_made")
        self.chain = self.sem("chain")
        self.exp_made = self.sem("exp_made")
        self.lse_made = self.sem("lse_made")
        self.index_made = self.sem("index_made")
        self.finished = self.sem("finished")

    def before_sync(self, sp):
        sp.dma_start(self.given[:, 0, :], self.logits.unsqueeze(0)).then_inc(self.given_in, 16)
        sp.dma_start(self.given[:, 1, :], self.u.unsqueeze(0)).then_inc(self.given_in, 16)
        sp.wait_ge(self.index_made, 1)
        self.chosen = sp.value_load(self.index[0:1, 0:1], min_val=0, max_val=self.experts - 1)
        rows_dma(sp, self.b_sb[:, :], self.b[bass.ds(self.chosen, 1), :].rearrange("o d -> (o d)").partition_broadcast(P),
                 self.b_in)

    def weight(self, sp, s):
        return self.weights[0][bass.ds(self.chosen, 1)].rearrange("o c d -> (o c) d")

    def before_scalar(self, act):
        nc = self.nc
        act.wait_ge(self.given_in, 32)
        nc.scalar.activation(self.logs[:, 0, :], self.given[:, 1, :], ACT.Ln).then_inc(self.log_made, 1)
        act.wait_ge(self.log_made, 1)
        nc.scalar.activation(self.logs[:, 1, :], self.logs[:, 0, :], ACT.Ln, scale=-1.0).then_inc(self.log_made, 1)
        act.wait_ge(self.chain, 2)
        nc.scalar.activation(self.expo[:, :], self.given[:, 0, :], ACT.Exp, bias=self.small[:, 1:2],
                             accum_out=self.small[:, 2:3]).then_inc(self.exp_made, 1)
        act.wait_ge(self.exp_made, 1)
        nc.scalar.activation(self.small[:, 3:4], self.small[:, 2:3], ACT.Ln).then_inc(self.lse_made, 1)

    def before_vector(self, dve):
        nc = self.nc
        super().before_vector(dve)
        dve.wait_ge(self.given_in, 32)
        nc.vector.reduce_max(self.small[:, 0:1], self.given[:, 0, :], AXX).then_inc(self.chain, 1)
        dve.wait_ge(self.chain, 1)
        nc.vector.tensor_scalar(self.small[:, 1:2], self.small[:, 0:1], -1.0, None, ALU.mult).then_inc(self.chain, 1)
        dve.wait_ge(self.lse_made, 1)
        nc.vector.tensor_scalar(self.score[:, 0, :], self.given[:, 0, :], self.small[:, 0:1], self.small[:, 3:4],
                                ALU.subtract, ALU.subtract).then_inc(self.chain, 1)
        dve.wait_ge(self.chain, 3)
        nc.vector.tensor_tensor(self.score[:, 1, :], self.score[:, 0, :], self.logs[:, 1, :], ALU.subtract
                                ).then_inc(self.chain, 1)
        dve.wait_ge(self.chain, 4)
        nc.vector.max(self.best[:, :], self.score[:, 1, :]).then_inc(self.chain, 1)
        dve.wait_ge(self.chain, 5)
        nc.vector.max_index(self.index[:, :], self.best[:, :], self.score[:, 1, :]).then_inc(self.index_made, 1)

    def finish_vector(self, dve, turn, s):
        nc, b, t = self.nc, turn.slot(2), turn.t(1)
        if turn.known() == 0:
            dve.wait_ge(self.b_in, ROWS_SEM)
        dve.wait_ge(self.multiplied, t)
        nc.vector.tensor_tensor(self.sums[:, b, :], self.acc[0:P, b, :], self.b_sb[:, :], ALU.add
                                ).then_inc(self.acc_read, 1)
        self.output_free(dve, "y", turn)
        dve.wait_ge(self.acc_read, t)
        nc.vector.tensor_tensor(self.out["y"][:, b, :], self.sums[:, b, :], self.inp["x"][:, turn.slot(4), :], ALU.add
                                ).then_inc(self.finished, 1)

    def output_ready(self, sp, name, turn):
        sp.wait_ge(self.finished, turn.t(1))


def program(nc, a, out):
    with ExitStack() as ctx:
        sem = Semaphores(nc)

        def scratch(name, shape, dt=F32):
            return nc.dram_tensor(name, shape, dt).ap()

        key_rows = scratch("key_rows", (EDGES,))
        counts = scratch("counts", (CELLS, 1), U16)
        counts2 = counts[0:NODES * NODES, :].rearrange("(d s) o -> d (s o)", s=NODES)
        xp = scratch("xp", (NODES, D))
        scores = scratch("scores", (NODES, 2 * HEADS))
        score_rows = scratch("score_rows", (HEADS, NODES))
        x1 = scratch("x1", (NODES + 1, D))
        r, k = scratch("r", (NODES, D)), scratch("k", (NODES, D))
        x2, x3 = scratch("x2", (NODES, D)), scratch("x3", (NODES, D))
        h_hi, h_lo = scratch("h_hi", (NODES, D)), scratch("h_lo", (NODES, D))

        ident = ctx.enter_context(nc.sbuf_tensor("ident", [128, 128], F32))
        dinv = ctx.enter_context(nc.sbuf_tensor("dinv", [P, NB], F32))
        ident_zero, ident_made = sem("ident_zero"), sem("ident_made")
        with nc.Block() as block:
            @block.gpsimd
            def _(pool):
                make_identity(nc, ident, ident_made, ident_zero)
                pool.wait_ge(ident_made, 1)
        sem.end_stage()

        build_counts(nc, sem, ident, a["src"], a["dst"], key_rows, counts)
        sem.end_stage()
        GatProject(nc, sem, ident, a["x"], a["L0_gnn_W"], a["L0_gnn_att_src"], a["L0_gnn_att_dst"], xp,
                   scores).run()
        sem.end_stage()
        attend(nc, sem, ident, a["x"], xp, scores, score_rows, counts, a["L0_gnn_bias"], x1)
        sem.end_stage()
        Mix(nc, sem, ident, x1, a["L0_ffn_W_r"], a["L0_ffn_W_k"], a["L0_ffn_mu_r"], a["L0_ffn_mu_k"], r, k).run()
        sem.end_stage()
        Value(nc, sem, ident, k, r, x1, a["L0_ffn_W_v"], counts2, x2, dinv).run()
        sem.end_stage()
        GcnProject(nc, sem, ident, x2, a["L1_gnn_W"], a["L1_gnn_b"], dinv, h_hi, h_lo).run()
        sem.end_stage()
        propagate(nc, sem, h_hi, h_lo, counts, dinv, x2, x3)
        sem.end_stage()
        Expert(nc, sem, ident, x3, a["L1_ffn_W"], a["L1_ffn_b"], a["L1_ffn_logits"], a["L1_ffn_u"], out).run()
        sem.end_stage()


INPUTS = ["x", "src", "dst", "L0_gnn_W", "L0_gnn_att_src", "L0_gnn_att_dst", "L0_gnn_bias", "L0_ffn_W_r", "L0_ffn_W_k",
          "L0_ffn_W_v", "L0_ffn_mu_r", "L0_ffn_mu_k", "L1_gnn_W", "L1_gnn_b", "L1_ffn_W", "L1_ffn_b", "L1_ffn_logits",
          "L1_ffn_u"]
TURNED = ["L0_ffn_W_r", "L0_ffn_W_k", "L0_ffn_W_v", "L1_gnn_W"]


def kernel(**inputs):
    import numpy as np
    import concourse.bacc as bacc
    from concourse.bass_utils import run_bass_kernel_spmd

    nc = bacc.Bacc("TRN2", target_bir_lowering=False, num_devices=1)
    arrays, aps = {}, {}
    for name in INPUTS:
        value = np.asarray(inputs[name])
        value = np.ascontiguousarray(value.T if name in TURNED else value)
        arrays["in_" + name] = value
        aps[name] = nc.dram_tensor("in_" + name, value.shape, mybir.dt.from_np(value.dtype), kind="ExternalInput").ap()
    out = nc.dram_tensor("out_x", (NODES, D), F32, kind="ExternalOutput").ap()
    program(nc, aps, out)
    result = run_bass_kernel_spmd(nc, [arrays], core_ids=[0])
    return result.results[0]["out_x"]
```

```python
import concourse.bass as bass
from concourse import mybir
from contextlib import ExitStack

F32 = mybir.dt.float32
F32R = mybir.dt.float32r
BF16 = mybir.dt.bfloat16
U16 = mybir.dt.uint16
U32 = mybir.dt.uint32
I32 = mybir.dt.int32
ALU = mybir.AluOpType
ACT = mybir.ActivationFunctionType
AXX = mybir.AxisListType.X

NODES = 3125
EDGES = 53125
D = 1024
P = 125
NB = NODES // P
KC = D // 128
HALF = 512
HEADS = 4
C = D // HEADS
SLOPE = 0.2
EPS = 1e-5
WIDE = 112
ROWS_SEM = 32
MASKED = -3.0e38

EG = EDGES // P
SG = 5
STEPS = EG // SG
SE = SG * P
PART_MAX = 4096.0
EARLIER = 4096.0
SPARE = NODES * NODES
CELLS = NODES * (NODES + 1)
ZERO = 2048


def rows_dma(eng, out, in_, sem):
    eng.dma_start(out[0:WIDE], in_[0:WIDE]).then_inc(sem, 16)
    eng.dma_start(out[WIDE:P], in_[WIDE:P]).then_inc(sem, 16)


def hold(eng, held, sem, value):
    eng.wait_ge(sem, value)
    eng.sem_inc(held, 1)


def at(base, first):
    return base[bass.ds(first, P)] if not isinstance(first, int) else base[first:first + P]


class Semaphores:

    def __init__(self, nc):
        self.nc, self.taken = nc, []

    def __call__(self, name):
        self.taken.append(self.nc.alloc_semaphore(name=name))
        return self.taken[-1]

    def end_stage(self):
        self.nc.clear_and_free_semaphores(self.taken)
        self.nc.all_engine_barrier()
        self.taken = []


def make_identity(nc, ident, made, step):
    nc.gpsimd.memset(ident[:, :], 0.0).then_inc(step, 1)
    nc.gpsimd.wait_ge(step, 1)
    nc.gpsimd.affine_select(out=ident[:, :], in_=ident[:, :], compare_op=ALU.not_equal, fill=1.0, base=0,
                            pattern=[[-1, 128]], channel_multiplier=1).then_inc(made, 1)


class Step:

    def __init__(self, i, n):
        self.i, self.rest = i, n

    def n(self, plus=0):
        return self.i * STEPS_ROUND + (self.rest + plus)

    def known(self):
        return self.n() if isinstance(self.i, int) else None

    def buf(self):
        return self.rest % 2

    def use(self):
        return self.i * (STEPS_ROUND // 2) + (self.rest // 2 + 1)


STEPS_TILE = [4, 3, 4, 3]
STEPS_ROUND = sum(STEPS_TILE)


def steps_of(turn):
    if turn.known() == NB - 1:
        return [Step(0, STEPS - 1)]
    return [Step(turn.i, sum(STEPS_TILE[:turn.j]) + q) for q in range(STEPS_TILE[turn.j])]


class Counts:

    def __init__(self, stage, src, dst, key_rows, counts_flat):
        self.stage, self.nc, self.src, self.dst = stage, stage.nc, src, dst
        self.key_rows, self.counts_flat = key_rows, counts_flat

    def allocate(self):
        sb, sem = self.stage.sb, self.stage.sem
        self.zero = sb("zero", [P, ZERO], U16)
        self.one = sb("one", [P, NB], U16)
        self.src_i = sb("src_i", [P, EG], I32)
        self.dst_i = sb("dst_i", [P, EG], I32)
        self.key = sb("key", [P, EG], F32)
        self.key_t = sb("key_t", [P, 4, P], F32)
        self.weight = sb("weight", [P, SG, SE], F32)
        self.slot_i = sb("slot_i", [P, SG], I32)
        self.slot = sb("slot", [P, SG], F32)
        self.row = sb("row", [P, 2, SE], F32)
        self.equal = sb("equal", [P, SG, SE], BF16)
        self.mine = sb("mine", [P, 2, SG], F32)
        self.found = sb("found", [P, 2, SG], F32)
        self.first = sb("first", [P, 2, SG], F32)
        self.shifted = sb("shifted", [P, 2, SG], F32)
        self.chosen = sb("chosen", [P, 2, SG], F32)
        self.cell = sb("cell", [P, 2, SG], I32)
        self.add = sb("add", [P, 2, SG], U16)
        self.turned = self.stage.acc[0:P, 0, 0:512].rearrange("p (c q) -> p c q", c=4)

        self.edges_in = sem("edges_in")
        self.zero_made = sem("zero_made")
        self.zeroed = sem("zeroed")
        self.diagonal = sem("diagonal")
        self.keys_made = sem("keys_made")
        self.key_turned = sem("key_turned")
        self.key_copied = sem("key_copied")
        self.key_stored = sem("key_stored")
        self.weight_set = sem("weight_set")
        self.weight_made = sem("weight_made")
        self.slot_made = sem("slot_made")
        self.slot_cast = sem("slot_cast")
        self.row_in = [sem("row_in0"), sem("row_in1")]
        self.mine_made = sem("mine_made")
        self.compared = sem("compared")
        self.first_made = sem("first_made")
        self.shift_made = sem("shift_made")
        self.chosen_made = sem("chosen_made")
        self.cells_made = sem("cells_made")
        self.scattered = sem("scattered")
        self.issued = sem("issued")
        self.chunks = [(c, min(P, EG - c * P)) for c in range(4)]

    def start_sync(self, sp):
        cells = self.counts_flat.rearrange("(p n) o -> p (n o)", p=P)
        whole, rest = divmod(CELLS // P, ZERO)

        def clear(first, last):
            rows_dma(sp, cells[:, first * ZERO:last * ZERO].rearrange("p (a n) -> p a n", n=ZERO),
                     self.zero[:, :].unsqueeze(1).broadcast_to([P, last - first, ZERO]), self.zeroed)

        rows_dma(sp, self.src_i[:, :], self.src.rearrange("(p g) -> p g", p=P), self.edges_in)
        rows_dma(sp, self.dst_i[:, :], self.dst.rearrange("(p g) -> p g", p=P), self.edges_in)
        sp.wait_ge(self.zero_made, 2)
        clear(0, 8)
        sp.wait_ge(self.key_copied, 2)
        for c, n in self.chunks:
            sp.dma_start(self.key_rows[c * P * P:c * P * P + n * P].rearrange("(g p) -> g p", p=P),
                         self.key_t[0:n, c, :]).then_inc(self.key_stored, 16)
        clear(8, 10)
        sp.wait_ge(self.key_stored, 64)
        for n in range(2):
            self.load_row(sp, Step(0, n))
        clear(10, whole)
        rows_dma(sp, cells[:, whole * ZERO:whole * ZERO + rest], self.zero[:, 0:rest], self.zeroed)

    def diagonal_sync(self, sp):
        for n in range(2):
            self.step_sync(sp, Step(0, n))
        sp.wait_ge(self.zeroed, 4 * ROWS_SEM)
        diag = self.counts_flat[:, :].rearrange("(p b s) o -> p b (s o)", b=NB, s=NODES + 1)[:, :, 0:1]
        with self.nc.allow_non_contiguous_dma(reason="one cell of every row"):
            rows_dma(sp, diag, self.one[:, :].unsqueeze(2), self.diagonal)

    def load_row(self, sp, step):
        known = step.known()
        if known is None or known >= 2:
            sp.wait_ge(self.compared, step.n(-1))
        row = (self.key_rows[bass.ds(step.n() * SE, SE)] if known is None
               else self.key_rows[known * SE:(known + 1) * SE])
        rows_dma(sp, self.row[:, step.buf(), :], row.partition_broadcast(P), self.row_in[step.buf()])

    def step_sync(self, sp, step):
        if step.known() is None or step.known() + 2 < STEPS:
            self.load_row(sp, Step(step.i, step.rest + 2))

    def start_vector(self, dve):
        nc = self.nc
        nc.vector.memset(self.zero[:, :], 0).then_inc(self.zero_made, 1)
        nc.vector.memset(self.one[:, :], 1).then_inc(self.zero_made, 1)
        dve.wait_ge(self.edges_in, 2 * ROWS_SEM)
        nc.vector.scalar_tensor_tensor(out=self.key[:, :], in0=self.dst_i[:, :], scalar=float(NODES),
                                       in1=self.src_i[:, :], op0=ALU.mult, op1=ALU.add).then_inc(self.keys_made, 1)
        dve.wait_ge(self.slot_made, 1)
        nc.vector.tensor_copy(self.slot[:, :], self.slot_i[:, :]).then_inc(self.slot_cast, 1)
        dve.wait_ge(self.key_turned, 1)
        rest = EG - 3 * P
        nc.vector.tensor_copy(self.key_t[:, 0:3, :], self.turned[:, 0:3, 0:P]).then_inc(self.key_copied, 1)
        nc.vector.tensor_copy(self.key_t[0:rest, 3, :], self.turned[0:rest, 3, 0:P]).then_inc(self.key_copied, 1)
        dve.wait_ge(self.keys_made, 1)
        dve.wait_ge(self.slot_cast, 1)
        dve.wait_ge(self.weight_made, SG)
        for n in range(2):
            self.step_vector(dve, Step(0, n))

    def step_vector(self, dve, step):
        nc, b, known = self.nc, step.buf(), step.known()
        mine = (self.key[:, bass.ds(step.n() * SG, SG)] if known is None
                else self.key[:, known * SG:(known + 1) * SG])
        nc.vector.tensor_copy(self.mine[:, b, :], mine).then_inc(self.mine_made, 1)
        dve.wait_ge(self.mine_made, step.n(1))
        dve.wait_ge(self.row_in[b], step.use() * ROWS_SEM)
        for g in range(SG):
            last = nc.vector.scalar_tensor_tensor(out=self.equal[:, g, :], in0=self.row[:, b, :],
                                                  scalar=self.mine[:, b, g:g + 1], in1=self.weight[:, g, :],
                                                  op0=ALU.is_equal, op1=ALU.mult, accum_out=self.found[:, b, g:g + 1])
        last.then_inc(self.compared, 1)
        nc.vector.tensor_tensor(self.shifted[:, b, :], self.mine[:, b, :], self.slot[:, :], ALU.subtract
                                ).then_inc(self.shift_made, 1)
        dve.wait_ge(self.compared, step.n(1))
        nc.vector.tensor_scalar(self.first[:, b, :], self.found[:, b, :], EARLIER, None, ALU.is_lt
                                ).then_inc(self.first_made, 1)
        dve.wait_ge(self.first_made, step.n(1))
        dve.wait_ge(self.shift_made, step.n(1))
        nc.vector.tensor_tensor(self.chosen[:, b, :], self.shifted[:, b, :], self.first[:, b, :], ALU.mult
                                ).then_inc(self.chosen_made, 1)
        if known is None or known >= 2:
            dve.wait_ge(self.scattered, step.n(-1) * (16 * SG))
        nc.vector.tensor_tensor(self.add[:, b, :], self.found[:, b, :], self.first[:, b, :], ALU.mult)
        dve.wait_ge(self.chosen_made, step.n(1))
        nc.vector.tensor_tensor(self.cell[:, b, :], self.chosen[:, b, :], self.slot[:, :], ALU.add
                                ).then_inc(self.cells_made, 1)

    def start_gpsimd(self, pool):
        nc = self.nc
        nc.gpsimd.iota(self.slot_i[:, :], pattern=[[P, SG]], base=SPARE, channel_multiplier=1).then_inc(self.slot_made, 1)
        nc.gpsimd.memset(self.weight[:, :, :], EARLIER + 1.0).then_inc(self.weight_set, 1)
        pool.wait_ge(self.weight_set, 1)
        for g in range(SG):
            nc.gpsimd.affine_select(out=self.weight[:, g, :], in_=self.weight[:, g, :], compare_op=ALU.is_gt, fill=1.0,
                                    base=g * P, pattern=[[-1, SE]], channel_multiplier=1).then_inc(self.weight_made, 1)

    def step_gpsimd(self, pool, step):
        if step.known() == 0:
            pool.wait_ge(self.diagonal, ROWS_SEM)
        pool.wait_ge(self.cells_made, step.n(1))
        pool.sem_inc(self.issued, 1)
        if step.known() is None or step.known() >= 1:
            pool.wait_ge(self.scattered, step.n() * (16 * SG))
            pool.sem_inc(self.issued, 1)
        for g in range(SG):
            self.nc.gpsimd.indirect_dma_start(
                self.counts_flat, bass.IndirectOffsetOnAxis(self.cell[:, step.buf(), g:g + 1], 0),
                self.add[:, step.buf(), g:g + 1], None, compute_op=ALU.add).then_inc(self.scattered, 16)

    def start_tensor(self, pe):
        pe.wait_ge(self.keys_made, 1)
        for c, n in self.chunks:
            last = self.nc.tensor.transpose(self.turned[0:n, c, 0:P], self.key[:, c * P:c * P + n],
                                            self.stage.ident[0:P, 0:P])
        last.then_inc(self.key_turned, 1)
        pe.wait_ge(self.key_copied, 2)


class Turn:

    def __init__(self, i, j, unroll):
        self.i, self.j, self.unroll = i + j // unroll if j >= unroll else i, j % unroll, unroll

    def t(self, plus=0):
        return self.i * self.unroll + (self.j + plus)

    def after(self, n):
        return Turn(self.i, self.j + n, self.unroll)

    def slot(self, bufs):
        return self.j % bufs

    def use(self, bufs):
        return self.i * (self.unroll // bufs) + (self.j // bufs + 1)

    def row(self, step=P, plus=0):
        return self.i * (self.unroll * step) + (self.j * step + plus)

    def known(self):
        return self.i * self.unroll + self.j if isinstance(self.i, int) else None


UNROLL = 4
ROUNDS = (NB - 1) // UNROLL - 1


def all_tiles(eng, body):
    for j in range(UNROLL):
        body(Turn(0, j, UNROLL))
    with eng.Fori(1, ROUNDS) as i:
        for j in range(UNROLL):
            body(Turn(i, j, UNROLL))
    for t in range(ROUNDS * UNROLL, NB):
        body(Turn(t // UNROLL, t % UNROLL, UNROLL))


class Dense:
    weights, inputs, outputs = (), (), ()
    raw_bufs = 4
    ahead = 2
    out_bufs = 2

    def __init__(self, nc, sem, ident, tag):
        self.nc, self.ident, self.tag, self.make_sem = nc, ident, tag, sem

    def sem(self, name):
        return self.make_sem(f"{self.tag}_{name}")

    def sb(self, name, shape, dt):
        return self.ctx.enter_context(self.nc.sbuf_tensor(f"{self.tag}_{name}", shape, dt))

    def ps(self, name, shape, dt):
        return self.ctx.enter_context(self.nc.psum_tensor(f"{self.tag}_{name}", shape, dt))

    def allocate(self): pass
    def weight(self, sp, s): return self.weights[s]
    def before_sync(self, sp): pass
    def before_scalar(self, act): pass
    def before_vector(self, dve): pass
    def prepare_vector(self, dve, turn): pass
    def prepare_gpsimd(self, pool, turn): pass
    def finish_scalar(self, act, turn, s): pass
    def finish_vector(self, dve, turn, s): pass
    def beside_sync(self, sp, turn, part): pass
    def beside_vector(self, dve, turn, part): pass
    def before_gpsimd(self, pool): pass
    def before_tensor(self, pe): pass
    def after_sync(self, sp): pass
    def after_vector(self, dve): pass
    def after_gpsimd(self, pool): pass
    def after_tensor(self, pe): pass

    def slots(self, turn, s):
        S = len(self.weights)
        return turn.i * (UNROLL * S) + (turn.j * S + s + 1)

    def early(self, turn, s):
        return turn.known() is not None and turn.known() * len(self.weights) + s < 2

    def loaded(self, eng, name, turn):
        bufs = len(self.in_sem[name])
        eng.wait_ge(self.in_sem[name][turn.slot(bufs)], turn.use(bufs) * ROWS_SEM)

    def output_free(self, eng, name, turn):
        if turn.known() is None or turn.known() >= self.out_bufs:
            eng.wait_ge(self.out_sem[name][turn.slot(self.out_bufs)], (turn.use(self.out_bufs) - 1) * ROWS_SEM)

    def run(self):
        nc, S, tag = self.nc, len(self.weights), self.tag
        with ExitStack() as ctx:
            self.ctx = ctx
            sb, ps, own = self.sb, self.ps, self.sem
            w_hi = [sb(f"w_hi{s}", [128, KC, D], F32R) for s in range(S)]
            w_lo = [sb(f"w_lo{s}", [128, KC, D], F32R) for s in range(S)]
            R = self.raw_bufs
            w_raw = sb("w_raw", [128, R, D], F32)
            self.inp = {n: sb(n, [P, b, src.shape[-1]], src.dtype) for n, src, _, b in self.inputs}
            x_hi = sb("x_hi", [128, 2, KC, P], F32R)
            x_lo = sb("x_lo", [128, 2, KC, P], F32R)
            self.out = {n: sb(n + "_o", [P, self.out_bufs, dst.shape[-1]], dt) for n, dst, _, dt in self.outputs}
            self.turned = turned = ps("turned", [128, 2, KC, 128], F32)
            self.acc = acc = ps("acc", [128, 2, D], F32)

            raw_in = [own(f"raw_in{b}") for b in range(R)]
            w_hi_made = own("w_hi_made")
            w_lo_made = own("w_lo_made")
            self.in_sem = {n: [own(f"{n}_in{b}") for b in range(bufs)] for n, _, _, bufs in self.inputs}
            self.out_sem = {n: [own(f"{n}_out{b}") for b in range(self.out_bufs)] for n, _, _, _ in self.outputs}
            self.prepared = [own(f"prepared{s}") for s in range(S)]
            self.transposed = transposed = own("transposed")
            x_hi_made = own("x_hi_made")
            x_lo_made = own("x_lo_made")
            self.multiplied = multiplied = own("multiplied")
            self.acc_read = own("acc_read")
            self.allocate()

            def buf(turn, s):
                return (turn.j * S + s) % 2

            def following(turn, s):
                if s + 1 < S:
                    return turn, s + 1
                known = turn.known()
                return (turn.after(1), 0) if known is None or known + 1 < NB else None

            with nc.Block() as block:
                @block.sync
                def _(sp):
                    def load(tile, lead=None):
                        for name, src, first, bufs in self.inputs:
                            ahead = 3 if bufs == 4 else 2
                            turn = tile.after(ahead) if lead is None else tile.after(lead)
                            if (lead or 0) >= ahead or (turn.known() is not None and turn.known() >= NB):
                                continue
                            if turn.known() is None or turn.known() >= bufs:
                                self.input_free(sp, name, turn, bufs)
                            rows_dma(sp, self.inp[name][:, turn.slot(bufs), :], at(src, turn.row(plus=first)),
                                     self.in_sem[name][turn.slot(bufs)])

                    def store(turn):
                        for name, dst, first, dt in self.outputs:
                            self.output_ready(sp, name, turn)
                            tile = self.out[name][:, turn.slot(self.out_bufs), :]
                            rows_dma(sp, at(dst, turn.row(plus=first)), tile.bitcast(F32) if dt == F32R else tile,
                                     self.out_sem[name][turn.slot(self.out_bufs)])

                    load(Turn(0, 0, UNROLL), 0)
                    self.before_sync(sp)
                    for n in range(S * KC):
                        s, c = divmod(n, KC)
                        if n >= R:
                            sp.wait_ge(w_lo_made, n - R + 1)
                        sp.dma_start(w_raw[:, n % R, :],
                                     self.weight(sp, s)[c * 128:(c + 1) * 128, :]).then_inc(raw_in[n % R], 16)
                        if n < 2:
                            load(Turn(0, 0, UNROLL), n + 1)

                    def tile(turn):
                        load(turn)
                        self.beside_sync(sp, turn, 0)
                        self.beside_sync(sp, turn, 1)
                        store(turn)

                    all_tiles(sp, tile)
                    self.after_sync(sp)
                    for name in self.out:
                        for b in range(self.out_bufs):
                            sp.wait_ge(self.out_sem[name][b], ROWS_SEM * len(range(b, NB, self.out_bufs)))

                @block.scalar
                def _(act):
                    self.before_scalar(act)

                    def split(turn, s):
                        n, b = self.slots(turn, s), buf(turn, s)
                        act.wait_ge(transposed, n)
                        if not self.early(turn, s):
                            act.wait_ge(multiplied, n - 2)
                        nc.scalar.activation(x_hi[:, b, :, :], turned[:, b, :, 0:P], ACT.Copy).then_inc(x_hi_made, 1)

                    split(Turn(0, 0, UNROLL), 0)
                    for n in range(S * KC):
                        s, c = divmod(n, KC)
                        act.wait_ge(raw_in[n % R], 16 * (n // R + 1))
                        nc.scalar.activation(w_hi[s][:, c, :], w_raw[:, n % R, :], ACT.Copy).then_inc(w_hi_made, 1)

                    def tile(turn):
                        for s in range(S):
                            if following(turn, s):
                                split(*following(turn, s))
                            self.finish_scalar(act, turn, s)

                    all_tiles(act, tile)

                @block.vector
                def _(dve):
                    self.before_vector(dve)
                    self.prepare_vector(dve, Turn(0, 0, UNROLL))

                    def split(turn, s):
                        n, b = self.slots(turn, s), buf(turn, s)
                        dve.wait_ge(x_hi_made, n)
                        nc.vector.tensor_tensor(x_lo[:, b, :, :], turned[:, b, :, 0:P], x_hi[:, b, :, :].bitcast(F32),
                                                ALU.subtract).then_inc(x_lo_made, 1)

                    split(Turn(0, 0, UNROLL), 0)
                    for n in range(S * KC):
                        s, c = divmod(n, KC)
                        dve.wait_ge(w_hi_made, n + 1)
                        nc.vector.tensor_tensor(w_lo[s][:, c, :], w_raw[:, n % R, :], w_hi[s][:, c, :].bitcast(F32),
                                                ALU.subtract).then_inc(w_lo_made, 1)
                        if n == KC // 2 and self.ahead == 2:
                            self.prepare_vector(dve, Turn(0, 1, UNROLL))

                    def tile(turn):
                        for s in range(S):
                            prepares = s == 0 and (turn.known() is None or turn.known() + self.ahead < NB)
                            if prepares and self.ahead == 1:
                                self.prepare_vector(dve, turn.after(1))
                            if following(turn, s):
                                split(*following(turn, s))
                            self.beside_vector(dve, turn, 0)
                            if prepares and self.ahead == 2:
                                self.prepare_vector(dve, turn.after(2))
                            self.finish_vector(dve, turn, s)
                            self.beside_vector(dve, turn, 1)

                    all_tiles(dve, tile)
                    self.after_vector(dve)

                @block.gpsimd
                def _(pool):
                    self.before_gpsimd(pool)
                    all_tiles(pool, lambda turn: self.prepare_gpsimd(pool, turn))
                    self.after_gpsimd(pool)

                @block.tensor
                def _(pe):
                    def turn_over(turn, s):
                        n, b = self.slots(turn, s), buf(turn, s)
                        self.operand_ready(pe, turn, s)
                        if not self.early(turn, s):
                            pe.wait_ge(x_lo_made, n - 2)
                        for c in range(KC):
                            last = nc.tensor.transpose(turned[:, b, c, 0:P],
                                                       self.operand(turn, s)[:, c * 128:(c + 1) * 128],
                                                       self.ident[0:P, 0:P])
                        last.then_inc(transposed, 1)

                    def product(turn, s):
                        n, b = self.slots(turn, s), buf(turn, s)
                        pe.wait_ge(x_hi_made, n)
                        pe.wait_ge(x_lo_made, n)
                        if not self.early(turn, s):
                            pe.wait_ge(self.acc_read, n - 2)
                        for h in range(D // HALF):
                            cols = slice(h * HALF, (h + 1) * HALF)
                            for c in range(KC):
                                if turn.known() == 0 and h == 0:
                                    pe.wait_ge(w_lo_made, s * KC + c + 1)
                                for m, (x, w) in enumerate(((x_hi, w_hi[s]), (x_hi, w_lo[s]), (x_lo, w_hi[s]))):
                                    last = nc.tensor.matmul(acc[0:P, b, cols], x[:, b, c, :], w[:, c, cols],
                                                            start=(c == 0 and m == 0), stop=(c == KC - 1 and m == 2))
                        last.then_inc(multiplied, 1)

                    self.before_tensor(pe)
                    turn_over(Turn(0, 0, UNROLL), 0)

                    def tile(turn):
                        for s in range(S):
                            if following(turn, s):
                                turn_over(*following(turn, s))
                            product(turn, s)

                    all_tiles(pe, tile)
                    self.after_tensor(pe)


class Norm:

    def __init__(self, stage, name):
        self.stage, self.nc, self.name = stage, stage.nc, name
        self.stats = stage.sb(name + "_stats", [P, 2, 2, 6], F32)
        self.moments = stage.sb(name + "_moments", [P, 2, 2], F32)
        self.var = stage.sb(name + "_var", [P, 2, 1], F32)
        self.rstd = stage.sb(name + "_rstd", [P, 2, 1], F32)
        self.minus_half = stage.sb(name + "_minus_half", [P, 1], F32)
        self.half_set = stage.sem(name + "_half_set")
        self.stats_made = stage.sem(name + "_stats_made")
        self.moments_made = stage.sem(name + "_moments_made")
        self.var_made = stage.sem(name + "_var_made")
        self.rstd_made = stage.sem(name + "_rstd_made")
        self.passed = stage.sem(name + "_passed")

    def set_constants(self):
        self.nc.vector.memset(self.minus_half[:, :], -0.5).then_inc(self.half_set, 1)

    def rows_of(self, turn):
        return self.stage.inp[self.name][:, turn.slot(len(self.stage.in_sem[self.name])), :]

    def take_moments(self, dve, turn):
        nc, b, t = self.nc, turn.slot(2), turn.t(1)
        x = self.rows_of(turn)
        self.stage.loaded(dve, self.name, turn)
        for h in range(D // HALF):
            last = nc.vector.bn_stats(self.stats[:, b, h, :], x[:, h * HALF:(h + 1) * HALF])
        last.then_inc(self.stats_made, 1)
        dve.wait_ge(self.stats_made, t)
        dve.sem_inc(self.passed, 1)
        nc.vector.bn_aggr(self.moments[:, b, :], self.stats[:, b, :, :]).then_inc(self.moments_made, 1)
        dve.wait_ge(self.moments_made, t)
        nc.vector.tensor_scalar(self.var[:, b, :], self.moments[:, b, 1:2], EPS, None, ALU.add).then_inc(self.var_made, 1)

    def normalise(self, dve, turn, out, free=None):
        nc, b, t, x = self.nc, turn.slot(2), turn.t(1), self.rows_of(turn)
        dve.wait_ge(self.rstd_made, t)
        if free:
            free(dve, turn)
        return nc.vector.tensor_scalar(out, x, self.moments[:, b, 0:1], self.rstd[:, b, :], ALU.subtract,
                                       ALU.mult)

    def vector(self, dve, turn, out, free=None):
        self.take_moments(dve, turn)
        return self.normalise(dve, turn, out, free)

    def gpsimd(self, pool, turn):
        if turn.known() == 0:
            pool.wait_ge(self.half_set, 1)
        pool.wait_ge(self.var_made, turn.t(1))
        self.nc.gpsimd.tensor_tensor(self.rstd[:, turn.slot(2), :], self.var[:, turn.slot(2), :], self.minus_half[:, :],
                                     ALU.pow).then_inc(self.rstd_made, 1)


class NormalisedDense(Dense):

    def allocate(self):
        self.norm = Norm(self, "x")
        self.xn = self.sb("xn", [P, 2, D], F32)

    def before_vector(self, dve):
        self.norm.set_constants()

    def xn_free(self, dve, turn):
        if turn.known() is None or turn.known() >= 2:
            dve.wait_ge(self.transposed, turn.t(-1))

    def prepare_vector(self, dve, turn):
        self.norm.vector(dve, turn, self.xn[:, turn.slot(2), :], self.xn_free).then_inc(self.prepared[0], 1)

    def prepare_gpsimd(self, pool, turn):
        self.norm.gpsimd(pool, turn)

    def operand(self, turn, s):
        return self.xn[:, turn.slot(2), :]

    def operand_ready(self, pe, turn, s):
        pe.wait_ge(self.prepared[0], turn.t(1))

    def input_free(self, sp, name, turn, bufs):
        sp.wait_ge(self.finished, turn.t(1 - bufs))


class GatProject(NormalisedDense):

    def __init__(self, nc, sem, ident, x, w, att_src, att_dst, xp, scores, src, dst, key_rows, counts):
        super().__init__(nc, sem, ident, "gatp")
        self.weights = [w]
        self.inputs = [("x", x, 0, 4)]
        self.outputs = [("xp", xp, 0, F32), ("sc", scores, 0, F32)]
        self.att = (att_src, att_dst)
        self.counts = Counts(self, src, dst, key_rows, counts)

    def allocate(self):
        super().allocate()
        self.att_sb = self.sb("att", [P, 2, D], F32)
        self.junk = self.sb("junk", [P, 2, 2 * HEADS, C], BF16)
        self.att_in = self.sem("att_in")
        self.xp_made = self.acc_read
        self.finished = self.sem("finished")
        self.counts.allocate()

    def before_sync(self, sp):
        self.counts.start_sync(sp)
        for i in range(2):
            rows_dma(sp, self.att_sb[:, i, :], self.att[i].rearrange("h c -> (h c)").partition_broadcast(P), self.att_in)
        self.counts.diagonal_sync(sp)

    def finish_scalar(self, act, turn, s):
        b = turn.slot(2)
        act.wait_ge(self.multiplied, turn.t(1))
        self.output_free(act, "xp", turn)
        self.nc.scalar.activation(self.out["xp"][:, b, :], self.acc[0:P, b, :], ACT.Copy).then_inc(self.acc_read, 1)

    def finish_vector(self, dve, turn, s):
        nc, b = self.nc, turn.slot(2)
        if turn.known() == 0:
            dve.wait_ge(self.att_in, 2 * ROWS_SEM)
        dve.wait_ge(self.xp_made, turn.t(1))
        self.output_free(dve, "sc", turn)
        for i in range(2):
            for h in range(HEADS):
                last = nc.vector.tensor_tensor_reduce(out=self.junk[:, b, i * HEADS + h, :],
                                                      in0=self.out["xp"][:, b, h * C:(h + 1) * C],
                                                      in1=self.att_sb[:, i, h * C:(h + 1) * C], scale=1.0, scalar=0.0,
                                                      op0=ALU.mult, op1=ALU.add,
                                                      accum_out=self.out["sc"][:, b, i * HEADS + h:i * HEADS + h + 1])
        last.then_inc(self.finished, 1)

    def output_ready(self, sp, name, turn):
        sp.wait_ge(self.finished, turn.t(1))

    def beside_sync(self, sp, turn, part):
        if turn.known() == 0 and part == 0:
            return
        steps = steps_of(turn)
        for step in (steps[:2], steps[2:])[part]:
            self.counts.step_sync(sp, step)

    def before_vector(self, dve):
        super().before_vector(dve)
        self.counts.start_vector(dve)

    def beside_vector(self, dve, turn, part):
        steps = steps_of(turn)
        if turn.known() == 0:
            steps = steps[2:]
        for step in (steps[:2], steps[2:])[part]:
            self.counts.step_vector(dve, step)

    def before_gpsimd(self, pool):
        self.counts.start_gpsimd(pool)

    def prepare_gpsimd(self, pool, turn):
        steps = steps_of(turn)
        if turn.known() == 0:
            for n in range(2):
                self.norm.gpsimd(pool, turn.after(n))
        for step in steps[:2]:
            self.counts.step_gpsimd(pool, step)
        if turn.known() == 0:
            self.norm.gpsimd(pool, turn.after(2))
            for step in steps[2:]:
                self.counts.step_gpsimd(pool, step)
            steps = []
        if turn.known() is None or turn.known() + 3 < NB:
            self.norm.gpsimd(pool, turn.after(3))
        for step in steps[2:]:
            self.counts.step_gpsimd(pool, step)

    def prepare_vector(self, dve, turn):
        if turn.known() == 0:
            self.norm.take_moments(dve, turn)
        self.norm.normalise(dve, turn, self.xn[:, turn.slot(2), :], self.xn_free).then_inc(self.prepared[0], 1)
        if turn.known() is None or turn.known() + 1 < NB:
            self.norm.take_moments(dve, turn.after(1))

    def after_gpsimd(self, pool):
        pool.wait_ge(self.counts.scattered, STEPS * SG * 16)

    def before_tensor(self, pe):
        self.counts.start_tensor(pe)


CHUNKS = [4, 3, 3, 3, 3, 3, 3, 3]
START = [sum(CHUNKS[:c]) for c in range(len(CHUNKS) + 1)]
NC = len(CHUNKS)
BUFS = 4
LEAD = 3
PIECES = [(0, START[3]), (START[3], START[6]), (START[6], NB)]
PIECE_OF = [0, 0, 0, 1, 1, 1, 2, 2]
GROUPS = HEADS // 2
GW = 2 * C
SEEN = 3


class Block2:

    def __init__(self, g, i, k):
        self.g, self.i, self.k = g, i + k // 2 if k >= 2 else i, k % 2

    def next(self):
        return Block2(self.g, self.i, self.k + 1)

    def blocks(self):
        return self.g * NB + (self.i * 2 + (self.k + 1))

    def slots(self, j):
        return self.g * (2 * NB) + (self.i * 4 + (2 * self.k + j + 1))

    def chunks(self, j, c):
        return self.g * (2 * NB * NC) + (self.i * (4 * NC) + ((2 * self.k + j) * NC + c + 1))

    def use(self):
        return self.g * ((NB + 1) // 2 if self.k == 0 else NB // 2) + (self.i + 1)

    def index(self, scale, plus=0):
        return self.i * (2 * scale) + (self.k * scale + plus)


def passes(eng, number, start, body):
    for g in range(number):
        start(g)
        with eng.Fori(0, (NB - SEEN) // 2) as i:
            for k in range(2):
                body(Block2(g, i, k), SEEN)
        for left in reversed(range(SEEN)):
            b = NB - 1 - left
            body(Block2(g, b // 2, b % 2), left)


def attend(nc, sem, ident, x, xp, scores, score_rows, counts, bias, x1):
    with ExitStack() as ctx:
        def sb(name, shape, dt):
            return ctx.enter_context(nc.sbuf_tensor("att_" + name, shape, dt))

        def own(name):
            return sem("att_" + name)

        xp_sb = sb("xp", [P, NB, 2, C + 1], F32)
        srow = sb("srow", [P, 2, NODES], F32)
        cnt = sb("cnt", [P, NODES], U16)
        cnt_f = sb("cnt_f", [P, NODES], F32)
        gone = sb("gone", [P, NODES], BF16)
        wt = sb("wt", [P, 4, NODES], F32)
        flipped = sb("flipped", [P, BUFS, max(CHUNKS), P], F32)
        cols = sb("cols", [P, NB * 2 * HEADS], F32)
        bias_sb = sb("bias", [P, 2, C], F32)
        xin = sb("xin", [P, GW], F32)
        sums = sb("sums", [P, 2, C], F32)
        x1_sb = sb("x1", [P, GW], F32)
        a_dst = sb("a_dst", [P, 2, 2], F32)
        top = sb("top", [P, 2, 2], F32)
        raised = sb("raised", [P, 2, 2], F32)
        minus = sb("minus", [P, 2, 2], F32)
        shift = sb("shift", [P, 2, 2], F32)
        inv = sb("inv", [P, 2, 1], F32)
        picked = sb("picked", [P, HEADS, NB], F32)
        rows_sb = sb("rows", [NB, HEADS, P], F32)
        turned = ctx.enter_context(nc.psum_tensor("att_turned", [128, BUFS, 4, 128], F32))
        acc = ctx.enter_context(nc.psum_tensor("att_acc", [128, 2, 512], F32))

        cols_in = own("cols_in")
        picked_made = own("picked_made")
        rows_turned = own("rows_turned")
        rows_made = own("rows_made")
        rows_out = own("rows_out")
        set_up = own("set_up")
        zero_out = own("zero_out")
        rows_in = own("rows_in")
        xp_in = [own("xp_in0"), own("xp_in1")]
        bias_in = own("bias_in")
        cnt_in = own("cnt_in")
        x_in = own("x_in")
        x1_out = own("x1_out")
        counts_cast = own("counts_cast")
        held = own("held")
        passed = own("passed")
        a_dst_made = own("a_dst_made")
        gone_made = own("gone_made")
        top_made = own("top_made")
        raised_made = own("raised_made")
        minus_made = own("minus_made")
        shift_made = own("shift_made")
        scores_made = own("scores_made")
        leaky_made = own("leaky_made")
        exp_made = own("exp_made")
        weighted = own("weighted")
        chunk_turned = own("chunk_turned")
        chunk_flipped = own("chunk_flipped")
        chunk_done = own("chunk_done")
        inv_made = own("inv_made")
        sums_made = own("sums_made")
        finished = own("finished")
        counts2 = counts[0:NODES * NODES, :].rearrange("(d s) o -> d (s o)", s=NODES)

        with nc.Block() as block:
            @block.sync
            def _(sp):
                rows_dma(sp, cols[:, :].rearrange("p (b h) -> p b h", b=NB), scores.rearrange("(b p) h -> p b h", p=P),
                         cols_in)
                sp.wait_ge(set_up, 1)
                for h in range(2):
                    sp.dma_start(x1[0:1, h * GW:(h + 1) * GW].rearrange("o (k f) -> o k f", k=2), sums[0:1, :, :]
                                 ).then_inc(zero_out, 16)
                def load_rows(g):
                    hold(sp, held, top_made, g * (2 * NB) + 1)
                    rows_dma(sp, srow[:, :, :], score_rows[g * 2:g * 2 + 2].partition_broadcast(P), rows_in)

                def load_xp(g, j):
                    hold(sp, held, finished, g * (2 * NB) + j + 1)
                    rows_dma(sp, xp_sb[:, :, j, 0:C],
                             xp.rearrange("(b p) f -> p b f", p=P)[:, :, g * GW + j * C:g * GW + (j + 1) * C], xp_in[j])

                def load_bias(g):
                    hold(sp, held, finished, g * (2 * NB) + 2)
                    rows_dma(sp, bias_sb[:, :, :], bias[g * GW:(g + 1) * GW].rearrange("(h c) -> h c", h=2)
                             .partition_broadcast(P), bias_in)

                def load_counts(blk):
                    hold(sp, held, gone_made, blk.blocks())
                    hold(sp, held, counts_cast, blk.blocks())
                    rows_dma(sp, cnt[:, :], counts2[bass.ds(blk.index(P), P)], cnt_in)

                def load_x(blk):
                    hold(sp, held, finished, blk.blocks() * 2)
                    rows_dma(sp, xin[:, :], x[bass.ds(blk.index(P), P), bass.ds(blk.g * GW, GW)], x_in)

                load_counts(Block2(0, 0, 0))
                sp.wait_ge(rows_made, 1)
                sp.dma_start(score_rows.rearrange("h (b p) -> b h p", p=P), rows_sb[:, :, :]).then_inc(rows_out, 16)
                sp.wait_ge(rows_out, 16)
                sp.sem_inc(x1_out, ROWS_SEM)
                load_rows(0)
                load_xp(0, 0)

                def start(g):
                    load_xp(g, 1)
                    load_bias(g)
                    load_x(Block2(g, 0, 0))
                    load_counts(Block2(g, 0, 1))

                def body(blk, left):
                    follows = blk.g + 1 < GROUPS
                    if left >= 2:
                        load_counts(blk.next().next())
                    if left == 1 and follows:
                        load_rows(blk.g + 1)
                    if left == 0 and follows:
                        load_counts(Block2(blk.g + 1, 0, 0))
                        load_xp(blk.g + 1, 0)
                    hold(sp, held, finished, blk.slots(1) + 2)
                    rows_dma(sp, x1[bass.ds(blk.index(P, 1), P), bass.ds(blk.g * GW, GW)], x1_sb[:, :], x1_out)
                    if left >= 1:
                        load_x(blk.next())

                passes(sp, GROUPS, start, body)
                sp.wait_ge(zero_out, 32)
                sp.wait_ge(x1_out, ROWS_SEM * (1 + GROUPS * NB))

            @block.vector
            def _(dve):
                nc.vector.memset(sums[0:1, :, :], 0.0).then_inc(set_up, 1)
                dve.wait_ge(cols_in, ROWS_SEM)
                nc.vector.tensor_copy(picked[:, :, :], cols[:, :].rearrange("p (b h) -> p h b", b=NB)[:, 0:HEADS, :]
                                      ).then_inc(picked_made, 1)
                nc.vector.memset(xp_sb[:, :, :, C:C + 1], 1.0).then_inc(set_up, 1)
                dve.wait_ge(rows_turned, 1)
                nc.vector.tensor_copy(rows_sb[:, :, :], turned[0:NB, 0, :, 0:P]).then_inc(rows_made, 1)
                for s, credit in ((finished, 2), (gone_made, 1), (top_made, 1)):
                    dve.sem_inc(s, credit)
                dve.wait_ge(zero_out, 32)

                def bar(blk):
                    nc.vector.tensor_copy(a_dst[:, blk.k, :], cols[:, bass.ds(blk.index(2 * HEADS, HEADS) + blk.g * 2, 2)]
                                          ).then_inc(a_dst_made, 1)
                    dve.wait_ge(cnt_in, blk.blocks() * ROWS_SEM)
                    dve.wait_ge(top_made, blk.slots(0))
                    nc.vector.tensor_scalar(gone[:, :], cnt[:, :], 0.0, MASKED, ALU.is_equal, ALU.mult
                                            ).then_inc(gone_made, 1)

                def maximum(blk, j, again=False):
                    n, k = blk.slots(j), blk.k
                    dve.wait_ge(chunk_turned, (n + 2) * NC if again else n * NC)
                    dve.wait_ge(gone_made, blk.blocks() + 1)
                    dve.sem_inc(passed, 1)
                    nc.vector.tensor_tensor_reduce(out=wt[:, 2 * k + j, :], in0=srow[:, j, :], in1=gone[:, :], scale=1.0,
                                                   scalar=-3.4e38, op0=ALU.add, op1=ALU.max,
                                                   accum_out=top[:, k, j:j + 1]).then_inc(top_made, 1)
                    dve.wait_ge(top_made, n + 1)
                    dve.wait_ge(a_dst_made, blk.blocks())
                    nc.vector.tensor_tensor(raised[:, k, j:j + 1], top[:, k, j:j + 1], a_dst[:, k, j:j + 1], ALU.add
                                            ).then_inc(raised_made, 1)
                    dve.wait_ge(raised_made, n)
                    nc.vector.tensor_scalar(minus[:, k, j:j + 1], raised[:, k, j:j + 1], -1.0, None, ALU.mult
                                            ).then_inc(minus_made, 1)
                    dve.wait_ge(minus_made, n)
                    nc.vector.scalar_tensor_tensor(out=shift[:, k, j:j + 1], in0=raised[:, k, j:j + 1], scalar=-SLOPE,
                                                   in1=minus[:, k, j:j + 1], op0=ALU.mult, op1=ALU.min
                                                   ).then_inc(shift_made, 1)

                def leaky(blk, j):
                    w = wt[:, 2 * blk.k + j, :]
                    dve.wait_ge(scores_made, blk.slots(j))
                    nc.vector.scalar_tensor_tensor(out=w, in0=w, scalar=SLOPE, in1=w, op0=ALU.mult, op1=ALU.max
                                                   ).then_inc(leaky_made, 1)

                def finish(blk, j):
                    n, span = blk.slots(j), slice(j * C, (j + 1) * C)
                    dve.wait_ge(chunk_done, blk.chunks(j, NC - 1) + BUFS)
                    nc.vector.reciprocal(inv[:, j, :], acc[0:P, j, C:C + 1]).then_inc(inv_made, 1)
                    dve.wait_ge(inv_made, n)
                    dve.wait_ge(bias_in, (blk.g + 1) * ROWS_SEM)
                    nc.vector.scalar_tensor_tensor(out=sums[:, j, :], in0=acc[0:P, j, 0:C], scalar=inv[:, j, :],
                                                   in1=bias_sb[:, j, :], op0=ALU.mult, op1=ALU.add).then_inc(sums_made, 1)
                    dve.wait_ge(x_in, blk.blocks() * ROWS_SEM)
                    dve.wait_ge(x1_out, blk.blocks() * ROWS_SEM)
                    dve.wait_ge(sums_made, n)
                    nc.vector.scalar_tensor_tensor(out=x1_sb[:, span], in0=sums[:, j, :], scalar=0.0,
                                                   in1=xin[:, span], op0=ALU.max, op1=ALU.add).then_inc(finished, 1)

                def begin(g):
                    first = Block2(g, 0, 0)
                    dve.wait_ge(rows_in, (g + 1) * ROWS_SEM)
                    bar(first)
                    maximum(first, 0, again=g > 0)
                    leaky(first, 0)
                    maximum(first, 1, again=g > 0)

                def start(g):
                    first = Block2(g, 0, 0)
                    leaky(first, 1)
                    bar(first.next())
                    maximum(first.next(), 0)
                    leaky(first.next(), 0)

                def body(blk, left):
                    if left >= 1:
                        maximum(blk.next(), 1)
                        leaky(blk.next(), 1)
                    finish(blk, 0)
                    if left >= 2:
                        bar(blk.next().next())
                        maximum(blk.next().next(), 0)
                        leaky(blk.next().next(), 0)
                    if left == 0 and blk.g + 1 < GROUPS:
                        begin(blk.g + 1)
                    finish(blk, 1)

                begin(0)
                passes(dve, GROUPS, start, body)

            @block.scalar
            def _(act):
                act.sem_inc(chunk_flipped, BUFS)
                act.sem_inc(counts_cast, 1)

                def cast(blk):
                    act.wait_ge(cnt_in, blk.blocks() * ROWS_SEM)
                    act.wait_ge(weighted, blk.slots(0) * 3 - 2)
                    nc.scalar.activation(cnt_f[:, :], cnt[:, :], ACT.Copy).then_inc(counts_cast, 1)

                def add_dst(blk, j):
                    w = wt[:, 2 * blk.k + j, :]
                    act.wait_ge(top_made, blk.slots(j) + 1)
                    act.wait_ge(a_dst_made, blk.blocks())
                    nc.scalar.activation(w, w, ACT.Identity, bias=a_dst[:, blk.k, j:j + 1]).then_inc(scores_made, 1)

                def exp(blk, j):
                    w = wt[:, 2 * blk.k + j, :]
                    act.wait_ge(leaky_made, blk.slots(j))
                    act.wait_ge(shift_made, blk.slots(j))
                    nc.scalar.activation(w, w, ACT.Exp, bias=shift[:, blk.k, j:j + 1]).then_inc(exp_made, 1)

                def flip(blk, j, c):
                    n = blk.chunks(j, c)
                    act.wait_ge(chunk_turned, n + 4 * NC)
                    act.wait_ge(chunk_done, n)
                    nc.scalar.activation(flipped[:, c % BUFS, 0:CHUNKS[c], :], turned[0:P, c % BUFS, 0:CHUNKS[c], 0:P],
                                         ACT.Copy).then_inc(chunk_flipped, 1)

                def begin(g):
                    add_dst(Block2(g, 0, 0), 0)
                    cast(Block2(g, 0, 0))

                def start(g):
                    first = Block2(g, 0, 0)
                    exp(first, 0)
                    add_dst(first, 1)
                    exp(first, 1)
                    add_dst(first.next(), 0)

                def body(blk, left):
                    for j in range(2):
                        for c in range(NC):
                            flip(blk, j, c)
                            if c == 1 and j == 0 and left >= 1:
                                cast(blk.next())
                            if c == 2 and left >= 1:
                                exp(blk.next(), j)
                            if c == 5 and j == 0 and left >= 1:
                                add_dst(blk.next(), 1)
                            if c == 5 and j == 1 and left >= 2:
                                add_dst(blk.next().next(), 0)
                            if c == 5 and j == 1 and left == 0 and blk.g + 1 < GROUPS:
                                begin(blk.g + 1)

                begin(0)
                passes(act, GROUPS, start, body)

            @block.gpsimd
            def _(pool):
                pool.sem_inc(weighted, 1)

                def weigh(blk, j):
                    pool.wait_ge(exp_made, blk.slots(j))
                    pool.wait_ge(counts_cast, blk.blocks() + 1)
                    for b0, b1 in PIECES:
                        w = wt[:, 2 * blk.k + j, b0 * P:b1 * P]
                        nc.gpsimd.tensor_tensor(w, w, cnt_f[:, b0 * P:b1 * P], ALU.mult).then_inc(weighted, 1)

                def body(blk, left):
                    weigh(blk, 0)
                    weigh(blk, 1)

                passes(pool, GROUPS, lambda g: None, body)

            @block.tensor
            def _(pe):
                pe.wait_ge(picked_made, 1)
                for h in range(HEADS):
                    last_t = nc.tensor.transpose(turned[0:NB, 0, h, 0:P], picked[:, h, :], ident[0:P, 0:P])
                last_t.then_inc(rows_turned, 1)
                pe.wait_ge(rows_made, 1)
                pe.wait_ge(set_up, 2)
                pe.sem_inc(chunk_turned, 4 * NC)
                pe.sem_inc(chunk_done, BUFS)

                def turn_over(blk, j, c):
                    n = blk.chunks(j, c)
                    pe.wait_ge(weighted, (blk.slots(j) - 1) * 3 + (PIECE_OF[c] + 2))
                    pe.wait_ge(chunk_flipped, n)
                    for b in range(CHUNKS[c]):
                        last = nc.tensor.transpose(turned[0:P, c % BUFS, b, 0:P],
                                                   wt[:, 2 * blk.k + j, (START[c] + b) * P:(START[c] + b + 1) * P],
                                                   ident[0:P, 0:P])
                    last.then_inc(chunk_turned, 1)

                def product(blk, j, c):
                    pe.wait_ge(chunk_flipped, blk.chunks(j, c) + BUFS)
                    if c == 0:
                        pe.wait_ge(finished, blk.slots(j))
                        pe.wait_ge(xp_in[j], (blk.g + 1) * ROWS_SEM)
                    for b in range(CHUNKS[c]):
                        last = nc.tensor.matmul(acc[0:P, j, 0:C + 1], flipped[:, c % BUFS, b, :], xp_sb[:, START[c] + b, j, :],
                                                start=(c == 0 and b == 0), stop=(c == NC - 1 and b == CHUNKS[c] - 1))
                    last.then_inc(chunk_done, 1)

                def start(g):
                    for c in range(LEAD):
                        turn_over(Block2(g, 0, 0), 0, c)

                def body(blk, left):
                    for j in range(2):
                        for c in range(NC):
                            if c + LEAD < NC:
                                turn_over(blk, j, c + LEAD)
                            elif j == 0:
                                turn_over(blk, 1, c + LEAD - NC)
                            elif left >= 1:
                                turn_over(blk.next(), 0, c + LEAD - NC)
                            product(blk, j, c)

                passes(pe, GROUPS, start, body)


class Mix(Dense):
    raw_bufs, ahead, out_bufs = 3, 1, 1

    def __init__(self, nc, sem, ident, x1, wr, wk, mu_r, mu_k, r, k):
        super().__init__(nc, sem, ident, "mix")
        self.weights = [wr, wk]
        self.inputs = [("x", x1, 1, 2), ("prev", x1, 0, 2)]
        self.outputs = [("r", r, 0, F32), ("k", k, 0, F32)]
        self.mu = (mu_r, mu_k)

    def allocate(self):
        self.norm = Norm(self, "x")
        self.norm_prev = Norm(self, "prev")
        self.mu_sb = self.sb("mu", [P, 2, D], F32)
        self.mixed = self.sb("mixed", [P, 2, D], F32)
        self.part = self.sb("part", [P, 2, D], F32)
        self.mu_in = self.sem("mu_in")
        self.normed = self.sem("normed")
        self.part_made = [self.sem("part_made0"), self.sem("part_made1")]
        self.main_made = [self.sem("main_made0"), self.sem("main_made1")]
        self.k_made = self.sem("k_made")

    def before_sync(self, sp):
        for i in range(2):
            rows_dma(sp, self.mu_sb[:, i, :], self.mu[i].partition_broadcast(P), self.mu_in)

    def before_vector(self, dve):
        self.norm.set_constants()
        self.norm_prev.set_constants()
        dve.wait_ge(self.mu_in, 2 * ROWS_SEM)

    def prepare_vector(self, dve, turn):
        nc, b, t = self.nc, turn.slot(2), turn.t(1)
        x, prev = self.inp["x"][:, b, :], self.inp["prev"][:, b, :]
        self.norm.vector(dve, turn, x).then_inc(self.normed, 1)
        self.norm_prev.vector(dve, turn, prev).then_inc(self.normed, 1)
        dve.wait_ge(self.normed, t * 2)
        if turn.known() is None or turn.known() >= 1:
            dve.wait_ge(self.transposed, t * 2 - 3)
        nc.vector.tensor_tensor(self.mixed[:, 0, :], x, self.mu_sb[:, 0, :], ALU.mult).then_inc(self.main_made[0], 1)
        nc.vector.scalar_tensor_tensor(out=self.part[:, 0, :], in0=self.mu_sb[:, 0, :], scalar=-1.0, in1=prev,
                                       op0=ALU.add, op1=ALU.mult).then_inc(self.part_made[0], 1)
        dve.wait_ge(self.main_made[0], t)
        dve.wait_ge(self.part_made[0], t)
        nc.vector.tensor_tensor(self.mixed[:, 0, :], self.mixed[:, 0, :], self.part[:, 0, :], ALU.subtract
                                ).then_inc(self.prepared[0], 1)

    def prepare_gpsimd(self, pool, turn):
        nc, b, t = self.nc, turn.slot(2), turn.t(1)
        x, prev = self.inp["x"][:, b, :], self.inp["prev"][:, b, :]
        self.norm.gpsimd(pool, turn)
        self.norm_prev.gpsimd(pool, turn)
        if turn.known() == 0:
            pool.wait_ge(self.mu_in, 2 * ROWS_SEM)
        pool.wait_ge(self.normed, t * 2)
        if turn.known() is None or turn.known() >= 1:
            pool.wait_ge(self.transposed, t * 2 - 2)
        nc.gpsimd.tensor_tensor(self.part[:, 1, :], x, prev, ALU.subtract).then_inc(self.part_made[1], 1)
        pool.wait_ge(self.part_made[1], t)
        nc.gpsimd.tensor_tensor(self.mixed[:, 1, :], self.part[:, 1, :], self.mu_sb[:, 1, :], ALU.mult
                                ).then_inc(self.main_made[1], 1)
        pool.wait_ge(self.main_made[1], t)
        nc.gpsimd.tensor_tensor(self.mixed[:, 1, :], self.mixed[:, 1, :], prev, ALU.add).then_inc(self.prepared[1], 1)

    def operand(self, turn, s):
        return self.mixed[:, s, :]

    def operand_ready(self, pe, turn, s):
        pe.wait_ge(self.prepared[s], turn.t(1))

    def input_free(self, sp, name, turn, bufs):
        for s in range(2):
            sp.wait_ge(self.prepared[s], turn.t(1 - bufs))

    def finish_scalar(self, act, turn, s):
        nc, b = self.nc, (turn.j * 2 + s) % 2
        name = "rk"[s]
        act.wait_ge(self.multiplied, self.slots(turn, s))
        self.output_free(act, name, turn)
        if s == 0:
            nc.scalar.activation(self.out["r"][:, 0, :], self.acc[0:P, b, :], ACT.Sigmoid).then_inc(self.acc_read, 1)
        else:
            nc.scalar.activation(self.out["k"][:, 0, :], self.acc[0:P, b, :], ACT.Relu).then_inc(self.acc_read, 1)
            act.wait_ge(self.acc_read, self.slots(turn, s))
            nc.scalar.activation(self.out["k"][:, 0, :], self.out["k"][:, 0, :], ACT.Square).then_inc(self.k_made, 1)

    def output_ready(self, sp, name, turn):
        if name == "r":
            sp.wait_ge(self.acc_read, self.slots(turn, 0))
        else:
            sp.wait_ge(self.k_made, turn.t(1))


class Value(Dense):

    def __init__(self, nc, sem, ident, k, r, x1, wv, counts, x2, dinv, many):
        super().__init__(nc, sem, ident, "val")
        self.weights = [wv]
        self.inputs = [("k", k, 0, 2), ("cnt", counts, 0, 2), ("r", r, 0, 4), ("x", x1, 1, 4)]
        self.outputs = [("x2", x2, 0, F32)]
        self.dinv, self.many = dinv, many

    def allocate(self):
        self.over = self.sb("over", [P, NB], F32)
        self.most = self.sb("most", [1, 1], F32)
        self.over_made = self.sem("over_made")
        self.over_summed = self.sem("over_summed")
        self.most_made = self.sem("most_made")
        self.many_made = self.sem("many_made")
        self.gated = self.sb("gated", [P, 2, D], F32)
        self.total = self.sb("total", [P, NODES], F32)
        self.ones = self.sb("ones", [P, 2], F32)
        self.degree = self.sb("degree", [P, NB], F32)
        self.half = self.sb("half", [P, NB], F32)
        self.consts_set = self.sem("consts_set")
        self.total_made = self.sem("total_made")
        self.finished = self.sem("finished")
        self.summed = self.sem("summed")
        self.degree_made = self.sem("degree_made")
        self.dinv_made = self.sem("dinv_made")
        self.degrees = self.ps_turned_view

    def ps_turned_view(self):
        return self.turned[0:P, 0, 0, 0:2 * NB].rearrange("p (b o) -> p b o", o=2)

    def before_vector(self, dve):
        self.nc.vector.memset(self.total[:, :], 0.0).then_inc(self.total_made, 1)
        self.nc.vector.memset(self.ones[:, :], 1.0).then_inc(self.consts_set, 1)
        self.nc.vector.memset(self.half[:, :], -0.5).then_inc(self.consts_set, 1)

    def operand(self, turn, s):
        return self.inp["k"][:, turn.slot(2), :]

    def operand_ready(self, pe, turn, s):
        self.loaded(pe, "k", turn)

    def input_free(self, sp, name, turn, bufs):
        if name == "k":
            sp.wait_ge(self.transposed, turn.t(1 - bufs))
        elif name == "cnt":
            sp.wait_ge(self.total_made, turn.t(1 - bufs) + 1)
        else:
            sp.wait_ge(self.finished, turn.t(1 - bufs))

    def finish_vector(self, dve, turn, s):
        nc, b, t = self.nc, turn.slot(2), turn.t(1)
        self.loaded(dve, "cnt", turn)
        dve.wait_ge(self.total_made, t)
        nc.vector.tensor_tensor(self.total[:, :], self.total[:, :], self.inp["cnt"][:, b, :], ALU.add
                                ).then_inc(self.total_made, 1)
        dve.wait_ge(self.multiplied, t)
        self.loaded(dve, "r", turn)
        nc.vector.tensor_tensor(self.gated[:, b, :], self.acc[0:P, b, :], self.inp["r"][:, turn.slot(4), :], ALU.mult
                                ).then_inc(self.acc_read, 1)
        self.loaded(dve, "x", turn)
        self.output_free(dve, "x2", turn)
        dve.wait_ge(self.acc_read, t)
        nc.vector.tensor_tensor(self.out["x2"][:, b, :], self.gated[:, b, :], self.inp["x"][:, turn.slot(4), :], ALU.add
                                ).then_inc(self.finished, 1)

    def output_ready(self, sp, name, turn):
        sp.wait_ge(self.finished, turn.t(1))

    def after_tensor(self, pe):
        pe.wait_ge(self.total_made, NB + 1)
        pe.wait_ge(self.consts_set, 2)
        for b in range(NB):
            last = self.nc.tensor.matmul(self.degrees()[:, b, :], self.total[:, b * P:(b + 1) * P], self.ones[:, :],
                                         start=True, stop=True)
        last.then_inc(self.summed, 1)
        pe.wait_ge(self.over_made, 1)
        self.nc.tensor.matmul(self.over_sums(), self.ones[:, :], self.over[:, :], start=True, stop=True
                              ).then_inc(self.over_summed, 1)

    def over_sums(self):
        return self.turned[0:2, 0, 1, 0:NB]

    def after_vector(self, dve):
        nc = self.nc
        dve.wait_ge(self.summed, 1)
        nc.vector.tensor_copy(self.degree[:, :], self.degrees()[:, :, 0]).then_inc(self.degree_made, 1)
        dve.wait_ge(self.degree_made, 1)
        nc.vector.tensor_scalar(self.over[:, :], self.degree[:, :], PART_MAX, None, ALU.is_gt).then_inc(self.over_made, 1)
        dve.wait_ge(self.over_summed, 1)
        nc.vector.reduce_max(self.most[:, :], self.over_sums()[0:1, :], AXX).then_inc(self.most_made, 1)
        dve.wait_ge(self.most_made, 1)
        nc.vector.tensor_copy(self.many[:, :], self.most[:, :]).then_inc(self.many_made, 1)
        dve.wait_ge(self.many_made, 1)

    def after_gpsimd(self, pool):
        pool.wait_ge(self.degree_made, 1)
        self.nc.gpsimd.tensor_tensor(self.dinv[:, :], self.degree[:, :], self.half[:, :], ALU.pow
                                     ).then_inc(self.dinv_made, 1)
        pool.wait_ge(self.dinv_made, 1)


class GcnProject(NormalisedDense):
    raw_bufs = KC

    def __init__(self, nc, sem, ident, x2, w, b, dinv, h):
        super().__init__(nc, sem, ident, "gcnp")
        self.weights = [w]
        self.inputs = [("x", x2, 0, 4)]
        self.outputs = [("h", h, 0, F32)]
        self.b, self.dinv = b, dinv

    def allocate(self):
        super().allocate()
        self.b_sb = self.sb("b", [P, D], F32)
        self.sums = self.sb("sums", [P, 2, D], F32)
        self.scale = self.sb("scale", [P, 2, 1], F32)
        self.b_in = self.sem("b_in")
        self.scale_made = self.sem("scale_made")
        self.finished = self.sem("finished")

    def before_sync(self, sp):
        rows_dma(sp, self.b_sb[:, :], self.b.partition_broadcast(P), self.b_in)

    def finish_vector(self, dve, turn, s):
        nc, b, t = self.nc, turn.slot(2), turn.t(1)
        if turn.known() is None or turn.known() >= 2:
            dve.wait_ge(self.finished, turn.t(-1))
        nc.vector.tensor_copy(self.scale[:, b, :], self.dinv[:, bass.ds(turn.t(), 1)]).then_inc(self.scale_made, 1)
        if turn.known() == 0:
            dve.wait_ge(self.b_in, ROWS_SEM)
        dve.wait_ge(self.multiplied, t)
        nc.vector.tensor_tensor(self.sums[:, b, :], self.acc[0:P, b, :], self.b_sb[:, :], ALU.add
                                ).then_inc(self.acc_read, 1)

    def finish_scalar(self, act, turn, s):
        b, t = turn.slot(2), turn.t(1)
        act.wait_ge(self.acc_read, t)
        act.wait_ge(self.scale_made, t)
        self.output_free(act, "h", turn)
        self.nc.scalar.activation(self.out["h"][:, b, :], self.sums[:, b, :], ACT.Copy, scale=self.scale[:, b, :]
                                  ).then_inc(self.finished, 1)

    def output_ready(self, sp, name, turn):
        sp.wait_ge(self.finished, turn.t(1))


PIECE = 5
PIECES_H = NB // PIECE


def propagate(nc, sem, h, counts, dinv, many, x2, x3):
    with ExitStack() as ctx:
        def sb(name, shape, dt):
            return ctx.enter_context(nc.sbuf_tensor("prop_" + name, shape, dt))

        def own(name):
            return sem("prop_" + name)

        hh = sb("hh", [P, NB, HALF], F32R)
        hl = sb("hl", [P, NB, HALF], F32R)
        cnt = sb("cnt", [P, 2, NB, P], U16)
        c_hi = sb("c_hi", [P, 2, NB, P], F32R)
        c_lo = sb("c_lo", [P, 2, NB, P], F32R)
        xin = sb("xin", [P, 2, HALF], F32)
        x3_sb = sb("x3", [P, 2, HALF], F32)
        h_raw = sb("h_raw", [P, 2, PIECE, HALF], F32)
        scale = sb("scale", [P, 2, 1], F32)
        acc = ctx.enter_context(nc.psum_tensor("prop_acc", [128, 2, HALF], F32))
        h_in = [own("h_in0"), own("h_in1")]
        h_hi_made = own("h_hi_made")
        h_lo_made = own("h_lo_made")
        held = own("held")
        cnt_in = [own("cnt_in0"), own("cnt_in1")]
        x_in = [own("x_in0"), own("x_in1")]
        x3_out = [own("x3_out0"), own("x3_out1")]
        hi_made = own("hi_made")
        lo_made = own("lo_made")
        scale_made = own("scale_made")
        multiplied = own("multiplied")
        finished = own("finished")
        counts3 = counts[0:NODES * NODES, :].rearrange("(b p s) o -> p b (s o)", p=P, s=NODES)

        with nc.Block() as block:
            @block.sync
            def _(sp):
                for b in range(2):
                    sp.sem_inc(x3_out[b], ROWS_SEM)

                def load_counts(blk):
                    hold(sp, held, lo_made, blk.blocks())
                    rows_dma(sp, cnt[:, blk.k, :, :], counts3[:, :, bass.ds(blk.index(P), P)], cnt_in[blk.k])

                def load_x(blk):
                    hold(sp, held, finished, blk.blocks())
                    rows_dma(sp, xin[:, blk.k, :], x2[bass.ds(blk.index(P), P), bass.ds(blk.g * HALF, HALF)], x_in[blk.k])

                def load_piece(q):
                    g, p = divmod(q, PIECES_H)
                    if q >= 2:
                        sp.wait_ge(h_lo_made, q - 1)
                    rows_dma(sp, h_raw[:, q % 2, :, :], h.rearrange("(b p) f -> p b f", p=P)[
                        :, p * PIECE:(p + 1) * PIECE, g * HALF:(g + 1) * HALF], h_in[q % 2])

                def begin(g):
                    hold(sp, held, lo_made, g * NB + 2)
                    load_counts(Block2(g, 0, 0))
                    for p in range(2):
                        load_piece(g * PIECES_H + p)

                def start(g):
                    for p in range(2, PIECES_H):
                        load_piece(g * PIECES_H + p)
                    load_counts(Block2(g, 0, 1))
                    hold(sp, held, finished, g * NB + 2)
                    load_x(Block2(g, 0, 0))
                    load_x(Block2(g, 0, 1))

                def body(blk, left):
                    if left >= 2:
                        load_counts(blk.next().next())
                    if left == 0 and blk.g == 0:
                        begin(1)
                    hold(sp, held, finished, blk.blocks() + 2)
                    rows_dma(sp, x3[bass.ds(blk.index(P), P), bass.ds(blk.g * HALF, HALF)], x3_sb[:, blk.k, :],
                             x3_out[blk.k])
                    if left >= 2:
                        load_x(blk.next().next())

                begin(0)
                passes(sp, 2, start, body)
                for b in range(2):
                    sp.wait_ge(x3_out[b], ROWS_SEM * (1 + 2 * ((NB + 1 - b) // 2)))

            @block.scalar
            def _(act):
                def start(g):
                    act.wait_ge(multiplied, g * NB + 2)
                    split(Block2(g, 0, 0))
                    for q in range(g * PIECES_H, (g + 1) * PIECES_H):
                        p = q % PIECES_H
                        act.wait_ge(h_in[q % 2], (q // 2 + 1) * ROWS_SEM)
                        nc.scalar.activation(hh[:, p * PIECE:(p + 1) * PIECE, :], h_raw[:, q % 2, :, :], ACT.Copy
                                             ).then_inc(h_hi_made, 1)

                def body(blk, left):
                    if left >= 1:
                        split(blk.next())

                def split(blk):
                    act.wait_ge(cnt_in[blk.k], blk.use() * ROWS_SEM)
                    act.wait_ge(multiplied, blk.blocks())
                    nc.scalar.activation(c_hi[:, blk.k, :, :], cnt[:, blk.k, :, :], ACT.Copy).then_inc(hi_made, 1)

                passes(act, 2, start, body)

            @block.vector
            def _(dve):
                for s in (lo_made, finished):
                    dve.sem_inc(s, 2)

                def split(blk):
                    dve.wait_ge(hi_made, blk.blocks())
                    nc.vector.tensor_tensor(c_lo[:, blk.k, :, :], cnt[:, blk.k, :, :], c_hi[:, blk.k, :, :].bitcast(F32),
                                            ALU.subtract).then_inc(lo_made, 1)

                def finish(blk):
                    k = blk.k
                    nc.vector.tensor_copy(scale[:, k, :], dinv[:, bass.ds(blk.index(1), 1)]).then_inc(scale_made, 1)
                    dve.wait_ge(multiplied, blk.blocks() + 2)
                    dve.wait_ge(x_in[k], blk.use() * ROWS_SEM)
                    dve.wait_ge(x3_out[k], blk.use() * ROWS_SEM)
                    dve.wait_ge(scale_made, blk.blocks())
                    nc.vector.scalar_tensor_tensor(out=x3_sb[:, k, :], in0=acc[0:P, k, :], scalar=scale[:, k, :],
                                                   in1=xin[:, k, :], op0=ALU.mult, op1=ALU.add).then_inc(finished, 1)

                def body(blk, left):
                    if left >= 1:
                        split(blk.next())
                    finish(blk)

                def start(g):
                    dve.wait_ge(finished, g * NB + 2)
                    split(Block2(g, 0, 0))
                    for q in range(g * PIECES_H, (g + 1) * PIECES_H):
                        p = q % PIECES_H
                        span = slice(p * PIECE, (p + 1) * PIECE)
                        dve.wait_ge(h_hi_made, q + 1)
                        nc.vector.tensor_tensor(hl[:, span, :], h_raw[:, q % 2, :, :], hh[:, span, :].bitcast(F32),
                                                ALU.subtract).then_inc(h_lo_made, 1)

                passes(dve, 2, start, body)

            @block.tensor
            def _(pe):
                pe.sem_inc(multiplied, 2)
                large = pe.value_load(many[0:1, 0:1], min_val=0, max_val=P)

                def part(blk, c, h, made, first=False, last=False):
                    for b in range(NB):
                        if b % PIECE == 0:
                            pe.wait_ge(made, blk.g * PIECES_H + b // PIECE + 1)
                        done = nc.tensor.matmul(acc[0:P, blk.k, :], c[:, blk.k, b, :], h[:, b, :],
                                                start=first and b == 0, stop=last and b == NB - 1)
                    return done

                def body(blk, left):
                    pe.wait_ge(lo_made, blk.blocks() + 2)
                    pe.wait_ge(finished, blk.blocks())
                    part(blk, c_hi, hh, h_hi_made, first=True)
                    with pe.If(large > 0):
                        part(blk, c_lo, hh, h_hi_made)
                    part(blk, c_hi, hl, h_lo_made, last=True).then_inc(multiplied, 1)

                passes(pe, 2, lambda g: hold(pe, held, finished, g * NB + 2), body)


class Expert(NormalisedDense):
    raw_bufs = KC

    def __init__(self, nc, sem, ident, x3, w, b, logits, u, out):
        super().__init__(nc, sem, ident, "exp")
        self.weights = [w]
        self.inputs = [("x", x3, 0, 4)]
        self.outputs = [("y", out, 0, F32)]
        self.b, self.logits, self.u = b, logits, u
        self.experts = w.shape[0]

    def allocate(self):
        super().allocate()
        E = self.experts
        self.b_sb = self.sb("b", [P, D], F32)
        self.sums = self.sb("sums", [P, 2, D], F32)
        self.given = self.sb("given", [1, 2, E], F32)
        self.logs = self.sb("logs", [1, 2, E], F32)
        self.small = self.sb("small", [1, 4], F32)
        self.expo = self.sb("expo", [1, E], F32)
        self.score = self.sb("score", [1, 2, E], F32)
        self.best = self.sb("best", [1, 8], F32)
        self.index = self.sb("index", [1, 8], U32)
        self.given_in = self.sem("given_in")
        self.b_in = self.sem("b_in")
        self.log_made = self.sem("log_made")
        self.chain = self.sem("chain")
        self.exp_made = self.sem("exp_made")
        self.lse_made = self.sem("lse_made")
        self.index_made = self.sem("index_made")
        self.finished = self.sem("finished")

    def before_sync(self, sp):
        sp.dma_start(self.given[:, 0, :], self.logits.unsqueeze(0)).then_inc(self.given_in, 16)
        sp.dma_start(self.given[:, 1, :], self.u.unsqueeze(0)).then_inc(self.given_in, 16)
        sp.wait_ge(self.index_made, 1)
        self.chosen = sp.value_load(self.index[0:1, 0:1], min_val=0, max_val=self.experts - 1)
        rows_dma(sp, self.b_sb[:, :], self.b[bass.ds(self.chosen, 1), :].rearrange("o d -> (o d)").partition_broadcast(P),
                 self.b_in)

    def weight(self, sp, s):
        return self.weights[0][bass.ds(self.chosen, 1)].rearrange("o c d -> (o c) d")

    def before_scalar(self, act):
        nc = self.nc
        act.wait_ge(self.given_in, 32)
        nc.scalar.activation(self.logs[:, 0, :], self.given[:, 1, :], ACT.Ln).then_inc(self.log_made, 1)
        act.wait_ge(self.log_made, 1)
        nc.scalar.activation(self.logs[:, 1, :], self.logs[:, 0, :], ACT.Ln, scale=-1.0).then_inc(self.log_made, 1)
        act.wait_ge(self.chain, 2)
        nc.scalar.activation(self.expo[:, :], self.given[:, 0, :], ACT.Exp, bias=self.small[:, 1:2],
                             accum_out=self.small[:, 2:3]).then_inc(self.exp_made, 1)
        act.wait_ge(self.exp_made, 1)
        nc.scalar.activation(self.small[:, 3:4], self.small[:, 2:3], ACT.Ln).then_inc(self.lse_made, 1)

    def before_vector(self, dve):
        nc = self.nc
        super().before_vector(dve)
        dve.wait_ge(self.given_in, 32)
        nc.vector.reduce_max(self.small[:, 0:1], self.given[:, 0, :], AXX).then_inc(self.chain, 1)
        dve.wait_ge(self.chain, 1)
        nc.vector.tensor_scalar(self.small[:, 1:2], self.small[:, 0:1], -1.0, None, ALU.mult).then_inc(self.chain, 1)
        dve.wait_ge(self.lse_made, 1)
        nc.vector.tensor_scalar(self.score[:, 0, :], self.given[:, 0, :], self.small[:, 0:1], self.small[:, 3:4],
                                ALU.subtract, ALU.subtract).then_inc(self.chain, 1)
        dve.wait_ge(self.chain, 3)
        nc.vector.tensor_tensor(self.score[:, 1, :], self.score[:, 0, :], self.logs[:, 1, :], ALU.subtract
                                ).then_inc(self.chain, 1)
        dve.wait_ge(self.chain, 4)
        nc.vector.max(self.best[:, :], self.score[:, 1, :]).then_inc(self.chain, 1)
        dve.wait_ge(self.chain, 5)
        nc.vector.max_index(self.index[:, :], self.best[:, :], self.score[:, 1, :]).then_inc(self.index_made, 1)

    def finish_vector(self, dve, turn, s):
        nc, b, t = self.nc, turn.slot(2), turn.t(1)
        if turn.known() == 0:
            dve.wait_ge(self.b_in, ROWS_SEM)
        dve.wait_ge(self.multiplied, t)
        nc.vector.tensor_tensor(self.sums[:, b, :], self.acc[0:P, b, :], self.b_sb[:, :], ALU.add
                                ).then_inc(self.acc_read, 1)
        self.output_free(dve, "y", turn)
        dve.wait_ge(self.acc_read, t)
        nc.vector.tensor_tensor(self.out["y"][:, b, :], self.sums[:, b, :], self.inp["x"][:, turn.slot(4), :], ALU.add
                                ).then_inc(self.finished, 1)

    def output_ready(self, sp, name, turn):
        sp.wait_ge(self.finished, turn.t(1))


def program(nc, a, out):
    with ExitStack() as ctx:
        sem = Semaphores(nc)

        def scratch(name, shape, dt=F32):
            return nc.dram_tensor(name, shape, dt).ap()

        key_rows = scratch("key_rows", (EDGES,))
        counts = scratch("counts", (CELLS, 1), U16)
        counts2 = counts[0:NODES * NODES, :].rearrange("(d s) o -> d (s o)", s=NODES)
        xp = scratch("xp", (NODES, D))
        scores = scratch("scores", (NODES, 2 * HEADS))
        score_rows = scratch("score_rows", (HEADS, NODES))
        x1 = scratch("x1", (NODES + 1, D))
        r, k = scratch("r", (NODES, D)), scratch("k", (NODES, D))
        x2, x3 = scratch("x2", (NODES, D)), scratch("x3", (NODES, D))
        h = scratch("h", (NODES, D))

        ident = ctx.enter_context(nc.sbuf_tensor("ident", [128, 128], F32))
        dinv = ctx.enter_context(nc.sbuf_tensor("dinv", [P, NB], F32))
        many = ctx.enter_context(nc.sbuf_tensor("many", [1, 1], I32))
        ident_zero, ident_made = sem("ident_zero"), sem("ident_made")
        with nc.Block() as block:
            @block.gpsimd
            def _(pool):
                make_identity(nc, ident, ident_made, ident_zero)
                pool.wait_ge(ident_made, 1)
        sem.end_stage()

        GatProject(nc, sem, ident, a["x"], a["L0_gnn_W"], a["L0_gnn_att_src"], a["L0_gnn_att_dst"], xp,
                   scores, a["src"], a["dst"], key_rows, counts).run()
        sem.end_stage()
        attend(nc, sem, ident, a["x"], xp, scores, score_rows, counts, a["L0_gnn_bias"], x1)
        sem.end_stage()
        Mix(nc, sem, ident, x1, a["L0_ffn_W_r"], a["L0_ffn_W_k"], a["L0_ffn_mu_r"], a["L0_ffn_mu_k"], r, k).run()
        sem.end_stage()
        Value(nc, sem, ident, k, r, x1, a["L0_ffn_W_v"], counts2, x2, dinv, many).run()
        sem.end_stage()
        GcnProject(nc, sem, ident, x2, a["L1_gnn_W"], a["L1_gnn_b"], dinv, h).run()
        sem.end_stage()
        propagate(nc, sem, h, counts, dinv, many, x2, x3)
        sem.end_stage()
        Expert(nc, sem, ident, x3, a["L1_ffn_W"], a["L1_ffn_b"], a["L1_ffn_logits"], a["L1_ffn_u"], out).run()
        sem.end_stage()


INPUTS = ["x", "src", "dst", "L0_gnn_W", "L0_gnn_att_src", "L0_gnn_att_dst", "L0_gnn_bias", "L0_ffn_W_r", "L0_ffn_W_k",
          "L0_ffn_W_v", "L0_ffn_mu_r", "L0_ffn_mu_k", "L1_gnn_W", "L1_gnn_b", "L1_ffn_W", "L1_ffn_b", "L1_ffn_logits",
          "L1_ffn_u"]
TURNED = ["L0_ffn_W_r", "L0_ffn_W_k", "L0_ffn_W_v", "L1_gnn_W"]


def kernel(**inputs):
    import numpy as np
    import concourse.bacc as bacc
    from concourse.bass_utils import run_bass_kernel_spmd

    nc = bacc.Bacc("TRN2", target_bir_lowering=False, num_devices=1)
    arrays, aps = {}, {}
    for name in INPUTS:
        value = np.asarray(inputs[name])
        value = np.ascontiguousarray(value.T if name in TURNED else value)
        arrays["in_" + name] = value
        aps[name] = nc.dram_tensor("in_" + name, value.shape, mybir.dt.from_np(value.dtype), kind="ExternalInput").ap()
    out = nc.dram_tensor("out_x", (NODES, D), F32, kind="ExternalOutput").ap()
    program(nc, aps, out)
    result = run_bass_kernel_spmd(nc, [arrays], core_ids=[0])
    return result.results[0]["out_x"]
```
